# Optimizing a Trainium2 kernel written in Bass

```python
import numpy as np
import jax
import jax.numpy as jnp

def _softmax(x, axis=-1):
    return jax.nn.softmax(x, axis=axis)

def _gelu(x):
    return jax.nn.gelu(x, approximate=True)

def _silu(x):
    return jax.nn.silu(x)

def _sigmoid(x):
    return jax.nn.sigmoid(x)

def _layernorm(x, axis=-1, eps=1e-05):
    m = jnp.mean(x, axis=axis, keepdims=True)
    v = jnp.var(x, axis=axis, keepdims=True)
    return (x - m) / jnp.sqrt(v + eps)

def _scatter_add(tgt, idx, src, axis=0):
    return tgt.at[idx].add(src)

def _segment_sum(src, seg, n):
    return jax.ops.segment_sum(src, seg, n)
kernel_name = 'mk_prb_d1_jaxref_r8_8e6943'

def setup_inputs(seed: int=0):
    np.random.seed(seed)
    _w = jnp.asarray

    def _L0_attn_setup():
        import jax, jax.numpy as jnp
        import numpy as np
        N_HEADS = 16
        HEAD_DIM = 64
        ROPE_THETA = 10000.0

        def _rope_cos_sin(seq_len, dim, theta):
            inv_freq = 1.0 / theta ** (jnp.arange(0, dim, 2, dtype=jnp.float32) / dim)
            pos = jnp.arange(seq_len, dtype=jnp.float32)
            freqs = pos[:, None] * inv_freq[None, :]
            emb = jnp.concatenate([freqs, freqs], axis=-1)
            return (jnp.cos(emb), jnp.sin(emb))

        def _rotate_half(x):
            d = x.shape[-1] // 2
            return jnp.concatenate([-x[..., d:], x[..., :d]], axis=-1)
        key = jax.random.key(seed)
        ks = jax.random.split(key, 6)
        B, S, D_MODEL, LATENT = (1, 512, 128, 64)
        q_dim = N_HEADS * HEAD_DIM
        sd = lambda fan_in: 1.0 / np.sqrt(fan_in)
        return {'x': jax.random.normal(ks[0], (B, S, D_MODEL), jnp.float32), 'wq': jax.random.normal(ks[1], (q_dim, D_MODEL), jnp.float32) * sd(D_MODEL), 'w_kv_down': jax.random.normal(ks[2], (LATENT, D_MODEL), jnp.float32) * sd(D_MODEL), 'w_k_up': jax.random.normal(ks[3], (q_dim, LATENT), jnp.float32) * sd(LATENT), 'w_v_up': jax.random.normal(ks[4], (q_dim, LATENT), jnp.float32) * sd(LATENT), 'wo': jax.random.normal(ks[5], (D_MODEL, q_dim), jnp.float32) * sd(q_dim)}
    _L0_attn_in = _L0_attn_setup()

    def _L0_ffn_setup():
        import jax, jax.numpy as jnp
        import numpy as np
        TOP_K = 4
        N_GROUP = 4
        TOPK_GROUP = 2
        ROUTED_SCALING = 2.5

        def _route(x, gate_weight):
            scores = jax.nn.sigmoid(x @ gate_weight.T)
            T, E = scores.shape
            gs = E // N_GROUP
            top2, _ = jax.lax.top_k(scores.reshape(T, N_GROUP, gs), 2)
            group_scores = top2.sum(-1)
            _, gidx = jax.lax.top_k(group_scores, TOPK_GROUP)
            gmask = jax.nn.one_hot(gidx, N_GROUP, dtype=jnp.float32).sum(1)
            smask = jnp.repeat(gmask, gs, axis=1) > 0.5
            masked = jnp.where(smask, scores, 0.0)
            topk_idx = jax.lax.top_k(masked, TOP_K)[1]
            topk_w = jnp.take_along_axis(scores, topk_idx, axis=1)
            topk_w = topk_w / (topk_w.sum(-1, keepdims=True) + 1e-20)
            topk_w = topk_w * ROUTED_SCALING
            combine = jnp.zeros((T, E), jnp.float32).at[jnp.arange(T)[:, None], topk_idx].add(topk_w)
            return combine
        key = jax.random.key(seed)
        ks = jax.random.split(key, 6)
        B, S, H = (2, 128, 128)
        E, I, Is = (16, 64, 256)
        g = lambda k, shape, scale: jax.random.normal(k, shape, dtype=jnp.float32) * scale
        return {'hidden_states': g(ks[0], (B, S, H), 1.0), 'gate_weight': g(ks[1], (E, H), 0.02), 'expert_up': g(ks[2], (E, H, I), 0.02), 'expert_down': g(ks[3], (E, I, H), 0.02), 'shared_up': g(ks[4], (H, Is), 0.02), 'shared_down': g(ks[5], (Is, H), 0.02)}
    _L0_ffn_in = _L0_ffn_setup()
    _d = {'L0_attn_x': _L0_attn_in['x'], 'L0_attn_wq': _L0_attn_in['wq'], 'L0_attn_w_kv_down': _L0_attn_in['w_kv_down'], 'L0_attn_w_k_up': _L0_attn_in['w_k_up'], 'L0_attn_w_v_up': _L0_attn_in['w_v_up'], 'L0_attn_wo': _L0_attn_in['wo'], 'L0_ffn_gate_weight': _L0_ffn_in['gate_weight'], 'L0_ffn_expert_up': _L0_ffn_in['expert_up'], 'L0_ffn_expert_down': _L0_ffn_in['expert_down'], 'L0_ffn_shared_up': _L0_ffn_in['shared_up'], 'L0_ffn_shared_down': _L0_ffn_in['shared_down']}
    _x0 = _d['L0_attn_x']
    _d['L0_attn_x'] = jax.random.normal(jax.random.fold_in(jax.random.key(seed), 1), (2, 1024, 128), dtype=_x0.dtype)
    del _x0
    return _d

def reference(L0_attn_x, L0_attn_wq, L0_attn_w_kv_down, L0_attn_w_k_up, L0_attn_w_v_up, L0_attn_wo, L0_ffn_gate_weight, L0_ffn_expert_up, L0_ffn_expert_down, L0_ffn_shared_up, L0_ffn_shared_down):

    def _L0_attn_ref(x, wq, w_kv_down, w_k_up, w_v_up, wo):
        import jax, jax.numpy as jnp
        import numpy as np
        N_HEADS = 16
        HEAD_DIM = 64
        ROPE_THETA = 10000.0

        def _rope_cos_sin(seq_len, dim, theta):
            inv_freq = 1.0 / theta ** (jnp.arange(0, dim, 2, dtype=jnp.float32) / dim)
            pos = jnp.arange(seq_len, dtype=jnp.float32)
            freqs = pos[:, None] * inv_freq[None, :]
            emb = jnp.concatenate([freqs, freqs], axis=-1)
            return (jnp.cos(emb), jnp.sin(emb))

        def _rotate_half(x):
            d = x.shape[-1] // 2
            return jnp.concatenate([-x[..., d:], x[..., :d]], axis=-1)
        B, S, _ = x.shape
        H, D = (N_HEADS, HEAD_DIM)
        q = jnp.einsum('bsd,qd->bsq', x, wq).reshape(B, S, H, D).transpose(0, 2, 1, 3)
        kv_latent = jnp.einsum('bsd,ld->bsl', x, w_kv_down)
        k = jnp.einsum('bsl,ql->bsq', kv_latent, w_k_up).reshape(B, S, H, D).transpose(0, 2, 1, 3)
        v = jnp.einsum('bsl,ql->bsq', kv_latent, w_v_up).reshape(B, S, H, D).transpose(0, 2, 1, 3)
        cos, sin = _rope_cos_sin(S, D, ROPE_THETA)
        cos = cos[None, None]
        sin = sin[None, None]
        q = q * cos + _rotate_half(q) * sin
        k = k * cos + _rotate_half(k) * sin
        scores = jnp.einsum('bhsd,bhtd->bhst', q, k) / jnp.sqrt(jnp.float32(D))
        causal = jnp.triu(jnp.full((S, S), -jnp.inf, dtype=jnp.float32), k=1)
        scores = scores + causal[None, None]
        probs = jax.nn.softmax(scores.astype(jnp.float32), axis=-1).astype(q.dtype)
        out = jnp.einsum('bhst,bhtd->bhsd', probs, v)
        out = out.transpose(0, 2, 1, 3).reshape(B, S, H * D)
        return jnp.einsum('bsq,dq->bsd', out, wo)

    def _L0_ffn_ref(hidden_states, gate_weight, expert_up, expert_down, shared_up, shared_down):
        import jax, jax.numpy as jnp
        import numpy as np
        TOP_K = 4
        N_GROUP = 4
        TOPK_GROUP = 2
        ROUTED_SCALING = 2.5

        def _route(x, gate_weight):
            scores = jax.nn.sigmoid(x @ gate_weight.T)
            T, E = scores.shape
            gs = E // N_GROUP
            top2, _ = jax.lax.top_k(scores.reshape(T, N_GROUP, gs), 2)
            group_scores = top2.sum(-1)
            _, gidx = jax.lax.top_k(group_scores, TOPK_GROUP)
            gmask = jax.nn.one_hot(gidx, N_GROUP, dtype=jnp.float32).sum(1)
            smask = jnp.repeat(gmask, gs, axis=1) > 0.5
            masked = jnp.where(smask, scores, 0.0)
            topk_idx = jax.lax.top_k(masked, TOP_K)[1]
            topk_w = jnp.take_along_axis(scores, topk_idx, axis=1)
            topk_w = topk_w / (topk_w.sum(-1, keepdims=True) + 1e-20)
            topk_w = topk_w * ROUTED_SCALING
            combine = jnp.zeros((T, E), jnp.float32).at[jnp.arange(T)[:, None], topk_idx].add(topk_w)
            return combine
        B, S, H = hidden_states.shape
        x = hidden_states.reshape(-1, H)
        combine = _route(x.astype(jnp.float32), gate_weight)
        up = jnp.einsum('th,ehi->eti', x, expert_up)
        down = jnp.einsum('eti,eih->eth', jax.nn.silu(up), expert_down)
        moe_out = jnp.einsum('te,eth->th', combine, down)
        shared = jax.nn.silu(x @ shared_up) @ shared_down
        return (moe_out + shared).reshape(B, S, H)
    x = L0_attn_x
    xn = _layernorm(x, axis=-1)
    x = x + _L0_attn_ref(xn, L0_attn_wq, L0_attn_w_kv_down, L0_attn_w_k_up, L0_attn_w_v_up, L0_attn_wo) + _L0_ffn_ref(xn, L0_ffn_gate_weight, L0_ffn_expert_up, L0_ffn_expert_down, L0_ffn_shared_up, L0_ffn_shared_down)
    return x

_drawn_inputs = setup_inputs


def setup_inputs(seed=0):
    import zlib

    import numpy as np

    out = dict(_drawn_inputs(seed))
    spreads = {}
    factors = {}
    for name, (base, spread) in spreads.items():
        noise = np.random.default_rng([zlib.crc32(name.encode()), seed]).standard_normal(out[name].shape)
        drawn = base * np.exp(spread * noise) if base else spread * noise
        out[name] = jnp.asarray(drawn.astype(out[name].dtype))
    for name, factor in factors.items():
        out[name] = (out[name] * factor).astype(out[name].dtype)
    return out
```

```python
from contextlib import ExitStack

import numpy as np

import concourse.bass as bass
from concourse import mybir

f32 = mybir.dt.float32
f32r = mybir.dt.float32r
bf16 = mybir.dt.bfloat16
ALU = mybir.AluOpType
ACT = mybir.ActivationFunctionType
AX = mybir.AxisListType

P = 128
B, S, D = 2, 1024, 128
HEADS, HD, LAT = 16, 64, 64
TILES = B * S // P
QB = S // P
QUADS = HEADS // 4
UNITS = B * QUADS
HALF = HD // 2
E, EI, SI = 16, 64, 256
CH = (E * EI + SI) // P
ECH = E * EI // P
GROUPS, TOPG, TOPK = 4, 2, 4
SCALING = 2.5
EPS = 1e-5
TB = 512

LONG, SHORT = [7, 6, 5, 4], [0, 1, 2, 3]
STEPS = 4 * QB
S_AHEAD, T_AHEAD = 5, 2


def step_of(m):
    m %= STEPS
    return m // (2 * QB), (SHORT if m % 2 else LONG)[m % (2 * QB) // 4], m % 4 // 2


def chunks_of(m):
    return 2 if step_of(m)[1] >= 4 else 1


CHUNKS = sum(chunks_of(m) for m in range(STEPS))
SECONDS = sum(chunks_of(m) - 1 for m in range(STEPS))


def chunks_before(m):
    return m // STEPS * CHUNKS + sum(chunks_of(n) for n in range(m % STEPS))


def seconds_before(m):
    return m // STEPS * SECONDS + sum(chunks_of(n) - 1 for n in range(m % STEPS))


BANK_USES = [(0, "R", 0), (1, "R", 1), (3, "R", 2), (4, "R", 3), (6, "R", 4), (7, "R", 5), (9, "R", 6), (10, "R", 7),
             (12, "O", (1, 0)), (14, "O", (1, 1)), (18, "O", (0, 0)), (20, "O", (0, 1))]
USES = len(BANK_USES)
ADD_AT, HI_AT, LO_AT = [(2, 3), (5, 6), (8, 9), (11, 12)], [4, 7, 10, 13], [5, 8, 11, 14]
Q_STACK_DMAS, K_STACK_DMAS = 2 * 4, 2 * 8


def block_kernel(nc, x, wq, w_down, w_kup, w_vup, wo, gate, e_up, e_down, s_up, s_down,
                 c_rope, c_ident, c_mask, c_sel, c_lower, out):
    ctx = ExitStack()
    with ctx:
        def sb(name, shape, dt, into=ctx):
            return into.enter_context(nc.sbuf_tensor(name, shape, dt))

        def sem(name):
            return ctx.enter_context(nc.semaphore(name))

        acc = sb("acc", [P, TILES, P], f32)
        rope = sb("rope", [P, 2, S], f32)
        xT = sb("xT", [P, B * S], f32)
        lT = sb("lT", [P, B * S], f32r)
        wqT = sb("wqT", [P, 2 * QUADS, P], f32)
        wkT = sb("wkT", [P, 2 * QUADS, 2, P], f32r)
        wq_now = sb("wq_now", [P, 2, P], f32)
        wk_now = sb("wk_now", [P, 2, 2, P], f32r)
        lat = sb("lat", [P, TILES, LAT], f32)
        lat_now = [sb(f"lat_now{p}", [P, QB, LAT], f32) for p in range(2)]
        mix = sb("mix", [P, HEADS // 2, P], f32)
        ident = sb("ident", [P, P], f32)
        identb = sb("identb", [P, P], bf16)
        maskb = sb("maskb", [P, P], bf16)
        roped = sb("roped", [P, 2, 2, 2, S], f32r)
        prod = sb("prod", [P, 2, 4, TB], f32)
        turned = sb("turned", [P, 2, 2, TB], f32)
        negmax = sb("negmax", [P, 4], f32)
        den = sb("den", [P, 4], f32)
        rden = sb("rden", [P, 4], f32)

        early = ExitStack()
        with early:
            hid = sb("hid", [P, CH, TB], f32, early)
            up = sb("up", [P, CH * P], f32, early)
            down = sb("down", [P, CH, P], f32, early)
            sel = sb("sel", [P, ECH, P], bf16, early)
            cT = sb("cT", [P, B * S], bf16, early)
            xn = sb("xn", [P, TILES, P], f32, early)
            wq_raw = sb("wq_raw", [P, 2 * QUADS, D], f32, early)
            wk_raw = sb("wk_raw", [P, 2 * QUADS, 2, LAT], f32, early)
            wv_raw = sb("wv_raw", [P, HEADS // 2, LAT], f32, early)
            wo_raw = sb("wo_raw", [P, HEADS // 2, P], f32, early)
            woT = sb("woT", [P, HEADS // 2, P], f32, early)
            comb3 = sb("comb3", [P, TILES, P], bf16, early)
            sel_raw = sb("sel_raw", [P, ECH * P], f32, early)
            lower = sb("lower", [P, E, E], f32, early)
            mask_raw = sb("mask_raw", [P, P], f32, early)
            gate_raw = sb("gate_raw", [E, D], f32, early)
            gateT = sb("gateT", [P, E], f32, early)
            wd_raw = sb("wd_raw", [P, D], f32, early)
            wdT = sb("wdT", [P, P], f32, early)
            stats = sb("stats", [P, TILES, 6], f32, early)
            mv = sb("mv", [P, TILES, 2], f32, early)
            std = sb("std", [P, 4, TILES], f32, early)
            route = sb("route", [P, 8, TILES * E], f32, early)
        probs = sb("probs", [P, 4, S], f32)
        probsT = sb("probsT", [P, 2, 2, S], f32)
        oT = [sb("oT0", [P, S], f32), None]
        qs = [sb(f"qs{n}", [P, S], f32r) for n in range(4)]
        kh = [sb(f"kh{n}", [P, S], f32r) for n in range(4)]
        kl = [sb(f"kl{n}", [P, S], f32r) for n in range(4)]
        oT[1] = sb("oT1", [P, S], f32)

        ps = ctx.enter_context(nc.psum_tensor("ps", [P, 8, TB], f32))
        sco = [ps[:, 0:2, :].rearrange("p a n -> p (a n)"), ps[:, 2:4, :].rearrange("p a n -> p (a n)")]
        PT0, OBANK, XBANK = 4, 6, 7

        in_x, in_consts, in_small, in_wq, in_wk, in_wv, in_rope, in_exp = map(
            sem, "in_x in_consts in_small in_wq in_wk in_wv in_rope in_exp".split())
        zeroed, ln_var, ln_std, ln_done, dve_own = map(sem, "zeroed ln_var ln_std ln_done dve_own".split())
        consts_cast, first_pe, first_act, first_dve = map(sem, "consts_cast first_pe first_act first_dve".split())
        sig_exp, comb_done, combT_pe, combT_done = map(sem, "sig_exp comb_done combT_pe combT_done".split())
        up_pe, silu_act, gated, down_pe, down_added = map(sem, "up_pe silu_act gated down_pe down_added".split())
        s_ready, max_ready, exp_done, rden_ready, p_ready = map(
            sem, "s_ready max_ready exp_done rden_ready p_ready".split())
        pt_ready, copied_act, copied_dve, pv_done, o_free = map(
            sem, "pt_ready copied_act copied_dve pv_done o_free".split())
        x_ready, x_free, prod_ready, turned_ready, hi_ready, lo_ready = map(
            sem, "x_ready x_free prod_ready turned_ready hi_ready lo_ready".split())
        in_stage, stored, divide_begun = sem("in_stage"), sem("stored"), sem("divide_begun")
        in_lat = [sem("in_lat0"), sem("in_lat1")]
        in_q = [sem("in_q0"), sem("in_q1")]
        in_k = [sem("in_k0"), sem("in_k1")]

        block = ctx.enter_context(nc.Block())

        @block.sync
        def _(sp):
            sp.dma_start(acc[:], x.rearrange("b (i p) d -> p (b i) d", p=P)).then_inc(in_x, 16)
            sp.dma_start(ident[:], c_ident).then_inc(in_consts, 16)
            for half in range(2):
                sp.dma_start(wd_raw[LAT * half:LAT * half + LAT, :], w_down).then_inc(in_small, 16)
            sp.dma_start(gate_raw[:], gate).then_inc(in_small, 16)
            wq_rows = wq.rearrange("(g h t j) d -> h t j g d", h=4, t=2, j=HALF)
            wk_rows = w_kup.rearrange("(g h t j) l -> h t j g l", h=4, t=2, j=HALF)
            for h in range(4):
                for t in range(2):
                    dst = wq_raw[HALF * h:HALF * h + HALF, :, :].rearrange("p (g t) d -> p t g d", t=2)[:, t]
                    sp.dma_start(dst, wq_rows[h, t]).then_inc(in_wq, 16)
            for h in range(4):
                for t in range(2):
                    for twice in range(2):
                        dst = wk_raw[HALF * h:HALF * h + HALF, :, twice, :].rearrange("p (g t) l -> p t g l", t=2)[:, t]
                        sp.dma_start(dst, wk_rows[h, t]).then_inc(in_wk, 16)
            sp.dma_start(wo_raw[:].rearrange("p c r -> p (c r)"), wo).then_inc(in_wv, 16)
            sp.dma_start(wv_raw[:], w_vup.rearrange("(c p) l -> p c l", p=P)).then_inc(in_wv, 16)
            sp.dma_start(mask_raw[:], c_mask).then_inc(in_consts, 16)
            sp.dma_start(sel_raw[:], c_sel).then_inc(in_consts, 16)
            sp.dma_start(lower[:], c_lower).then_inc(in_consts, 16)
            sp.dma_start(rope[:], c_rope).then_inc(in_rope, 16)
            sp.dma_start(up[:, 0:E * EI].rearrange("p (e i) -> p e i", i=EI),
                         e_up.rearrange("e h i -> h e i")).then_inc(in_exp, 16)
            sp.dma_start(up[:, E * EI:], s_up).then_inc(in_exp, 16)
            sp.dma_start(down[:, 0:ECH, :], e_down.rearrange("(c f) i h -> (f i) c h", f=2)).then_inc(in_exp, 16)
            sp.dma_start(down[:, ECH:, :], s_down.rearrange("(c p) h -> p c h", p=P)).then_inc(in_exp, 16)

            def stage_weights(n):
                g = n % QUADS
                sp.dma_start(wq_now[:], wqT[:, bass.ds(2 * g, 2), :]).then_inc(in_stage, 16)
                sp.dma_start(wk_now[:].bitcast(f32), wkT[:, bass.ds(2 * g, 2), :, :].bitcast(f32)).then_inc(in_stage, 16)

            def stage_latent(n, p):
                b = (n // QUADS) % B
                sp.dma_start(lat_now[p][:], lat[:, bass.ds(QB * b, QB), :]).then_inc(in_lat[p], 16)

            def stack_q(p):
                for a in range(2):
                    src = roped[HALF * (2 * p + a):HALF * (2 * p + a) + HALF, 0]
                    for h in range(2):
                        for t in range(2):
                            at = HD * h + HALF * t
                            sp.dma_start(qs[2 * p + a][at:at + HALF, :].bitcast(f32),
                                         src[:, h, t, :].bitcast(f32)).then_inc(in_q[p], 16)

            def stack_k(p):
                for a in range(2):
                    src = roped[HALF * (2 * p + a):HALF * (2 * p + a) + HALF, 1]
                    for h, dst in ((0, kh), (1, kl)):
                        for twice in range(2):
                            for t in range(2):
                                at = HD * twice + HALF * t
                                sp.dma_start(dst[2 * p + a][at:at + HALF, :].bitcast(f32),
                                             src[:, h, t, :].bitcast(f32)).then_inc(in_k[p], 16)

            sp.wait_ge(first_act, FIRST_ACT_LAT)
            sp.wait_ge(first_dve, FIRST_DVE_WK)
            stage_weights(0)
            for p in range(2):
                stage_latent(0, p)
            sp.wait_ge(x_ready, 8)
            stage_weights(1)
            sp.wait_ge(combT_pe, 1)
            sp.wait_ge(consts_cast, 3)
            sp.wait_ge(first_pe, FIRST_JOBS)
            sp.wait_ge(lo_ready, 4)
            for p in range(2):
                stack_q(p)
                stack_k(p)

            with sp.Fori(0, UNITS) as u:
                n = u + 1
                sp.wait_ge(lo_ready, u * 4 + 6)
                sp.wait_ge(s_ready, u * STEPS + 16)
                stack_q(0)
                sp.wait_ge(x_ready, u * USES + 8 + 8)
                stage_weights(n + 1)
                sp.wait_ge(pv_done, u * 16 + 8)
                stage_latent(n, 0)
                sp.wait_ge(lo_ready, u * 4 + 8)
                stack_k(0)
                sp.wait_ge(s_ready, u * STEPS + 32)
                stack_q(1)
                stack_k(1)
                sp.wait_ge(pv_done, u * 16 + 16)
                stage_latent(n, 1)

            sp.wait_ge(x_free, UNITS * USES + 8 + 2)
            sp.dma_start(out.rearrange("b (i p) d -> p (b i) d", p=P), acc[:]).then_inc(stored, 16)
            sp.wait_ge(stored, 16)

        @block.tensor
        def _(pe):
            def done(ins):
                ins.then_inc(first_pe, 1)

            pe.wait_ge(in_consts, 16 * 4)
            pe.wait_ge(in_small, 16 * 3)
            nc.tensor.transpose(ps[:, 0, 0:P], wd_raw[:], ident[:])
            done(nc.tensor.transpose(ps[:, 0, P:P + E], gate_raw[:], ident[0:E, 0:E]))
            pe.wait_ge(in_wq, 16 * 8)
            for half in range(2):
                for c in range(4):
                    last = nc.tensor.transpose(ps[:, 1 + half, c * P:(c + 1) * P], wq_raw[:, 4 * half + c, :], ident[:])
                done(last)
            pe.wait_ge(in_wk, 16 * 16)
            for half in range(2):
                for c in range(4):
                    last = nc.tensor.transpose(ps[:, 3 + half, c * P:(c + 1) * P],
                                               wk_raw[:, 4 * half + c, :, :].rearrange("p a l -> p (a l)"), ident[:])
                done(last)
            pe.wait_ge(in_wv, 16 * 2)
            for half in range(2):
                for c in range(4):
                    last = nc.tensor.transpose(ps[:, 5 + half, c * P:(c + 1) * P], wo_raw[:, 4 * half + c, :], ident[:])
                done(last)
            for b in range(4):
                pe.wait_ge(ln_done, 4 * (b + 1))
                pe.wait_ge(first_act, b + 1)
                if b == 3:
                    pe.wait_ge(first_dve, 1)
                for c in range(4):
                    last = nc.tensor.transpose(ps[:, b, c * P:(c + 1) * P], xn[:, 4 * b + c, :], ident[:])
                done(last)
            for c, bank in enumerate((4, 5, 6, 0)):
                pe.wait_ge(first_act, max(5 + c, 8 + c))
                if c == 0:
                    pe.wait_ge(first_dve, 2)
                done(nc.tensor.matmul(ps[:, bank, :], wdT[:], xT[:, c * TB:(c + 1) * TB], start=True, stop=True))
            pe.wait_ge(first_act, 11)
            for i in range(TILES):
                last = nc.tensor.matmul(ps[:, 1, i * E:(i + 1) * E], xT[:, i * P:(i + 1) * P], gateT[:],
                                        start=True, stop=True)
            done(last)
            for half in range(2):
                for i in range(QB):
                    last = nc.tensor.matmul(ps[:, 2 + half, i * LAT:(i + 1) * LAT],
                                            xT[:, (QB * half + i) * P:(QB * half + i + 1) * P], wdT[:, 0:LAT],
                                            start=True, stop=True)
                done(last)
            for half in range(2):
                pe.wait_ge(first_act, 12 + half)
                pe.wait_ge(first_dve, 3 + half)
                for c in range(4):
                    for a in range(2):
                        rows = slice(HD * a, HD * a + HD)
                        last = nc.tensor.matmul(ps[rows, 4 + half, c * P:(c + 1) * P], wv_raw[rows, 4 * half + c, :],
                                                woT[rows, 4 * half + c, :], start=True, stop=True)
                done(last)

            def rotary_product(n, r, use):
                ck, t = r % 4 // 2, r % 2
                cols = bass.ds((n // QUADS) % B * S + ck * TB, TB)
                if r == 0:
                    pe.wait_ge(in_stage, n * 32 + 32)
                pe.wait_ge(x_free, use)
                if r < 4:
                    last = nc.tensor.matmul(ps[:, XBANK, :], wq_now[:, t, :], xT[:, cols], start=True, stop=True)
                else:
                    nc.tensor.matmul(ps[:, XBANK, :], wk_now[:, t, 0, :], lT[:, cols], start=True, stop=False)
                    last = nc.tensor.matmul(ps[:, XBANK, :], wk_now[:, t, 1, :], lT[:, cols], start=False, stop=True)
                last.then_inc(x_ready, 1)

            pe.wait_ge(first_act, 15)
            pe.wait_ge(first_dve, 6)
            for r in range(8):
                if r == 0:
                    pe.wait_ge(in_stage, 32)
                if r:
                    pe.wait_ge(x_free, r)
                ck, t = r % 4 // 2, r % 2
                cols = slice(ck * TB, ck * TB + TB)
                if r < 4:
                    last = nc.tensor.matmul(ps[:, XBANK, :], wq_now[:, t, :], xT[:, cols], start=True, stop=True)
                else:
                    nc.tensor.matmul(ps[:, XBANK, :], wk_now[:, t, 0, :], lT[:, cols], start=True, stop=False)
                    last = nc.tensor.matmul(ps[:, XBANK, :], wk_now[:, t, 1, :], lT[:, cols], start=False, stop=True)
                last.then_inc(x_ready, 1)

            pe.wait_ge(comb_done, 1)
            pe.wait_ge(consts_cast, 3)
            pe.wait_ge(first_act, FIRST_ACT)
            for i in range(TILES):
                bank = ps[:, 5 + i // 8, :].bitcast(bf16)
                last = nc.tensor.transpose(bank[:, i % 8 * P:(i % 8 + 1) * P], comb3[:, i, :], identb[:])
            last.then_inc(combT_pe, 1)
            pe.wait_ge(combT_done, 1)
            pe.wait_ge(in_exp, 64)
            with pe.Fori(0, B * S // TB) as tb:
                cols = bass.ds(tb * TB, TB)
                for c in range(CH):
                    if c >= 2:
                        pe.wait_ge(gated, tb * ECH + c - 1)
                    last = nc.tensor.matmul(ps[:, c % 2, :], up[:, c * P:(c + 1) * P], xT[:, cols],
                                            start=True, stop=True)
                    if c < ECH:
                        last = nc.tensor.matmul(ps[:, 2 + c % 2, :], sel[:, c, :], cT[:, cols], start=True, stop=True)
                    last.then_inc(up_pe, 1)
                pe.wait_ge(gated, tb * ECH + ECH)
                pe.wait_ge(silu_act, tb * CH + CH)
                for i in range(TB // P):
                    for c in range(CH):
                        last = nc.tensor.matmul(ps[:, 4, i * P:(i + 1) * P], hid[:, c, i * P:(i + 1) * P],
                                                down[:, c, :], start=(c == 0), stop=(c == CH - 1))
                last.then_inc(down_pe, 1)
                pe.wait_ge(down_added, tb + 1)

            def scores(m, count):
                p, i, a = step_of(m)
                if m == 0 or m >= 2:
                    if count is not None:
                        pe.wait_ge(exp_done, count)
                n, width = 2 * p + a, (i + 1) * P
                q = qs[n][:, i * P:(i + 1) * P]
                out_ps = sco[m % 2]
                for lo in range(0, width, TB):
                    hi = min(lo + TB, max(width, lo + 2 * P))
                    nc.tensor.matmul(out_ps[:, lo:hi], q, kh[n][:, lo:hi], start=True, stop=False)
                    if lo <= i * P < hi:
                        nc.tensor.matmul(out_ps[:, i * P:(i + 1) * P], identb[:], maskb[:], start=False, stop=False)
                    last = nc.tensor.matmul(out_ps[:, lo:hi], q, kl[n][:, lo:hi], start=False, stop=True)
                last.then_inc(s_ready, 1)

            def transposes(m, u, probs_count):
                _, i, _ = step_of(m)
                pe.wait_ge(p_ready, probs_count)
                for x_ in range(chunks_of(m)):
                    k = chunks_before(m) + x_ - 2
                    if k >= 0:
                        by, base, per = copier_of(k)
                        pe.wait_ge(copied_dve if by else copied_act, u * per + base)
                    for kb in range(4 * x_, min(4 * x_ + 4, i + 1)):
                        bank = PT0 + (chunks_before(m) + x_) % 2
                        last = nc.tensor.transpose(ps[:, bank, kb % 4 * P:(kb % 4 + 1) * P],
                                                   probs[:, m % 4, kb * P:(kb + 1) * P], ident[:])
                    last.then_inc(pt_ready, 1)

            def products(m, u):
                p, i, _ = step_of(m)
                k = m // 4 * 2 + m % 2
                if k % 8 == 0:
                    pe.wait_ge(in_lat[p], u * 16 + 16)
                pe.wait_ge(o_free, u * 16 + k + 1)
                pe.wait_ge(copied_act, u * STEPS + m + 1)
                pe.wait_ge(copied_dve, u * SECONDS + seconds_before(m + 1))
                for kb in range(i + 1):
                    for a in range(2):
                        last = nc.tensor.matmul(ps[HD * a:HD * a + HD, OBANK, 0:P], lat_now[p][:, kb, :],
                                                probsT[:, m % 2, a, kb * P:(kb + 1) * P],
                                                start=(kb == 0), stop=(kb == i))
                last.then_inc(pv_done, 1)

            def project(p, half, m0, use):
                pe.wait_ge(x_free, use)
                for c in range(4):
                    i = 4 * half + c
                    last = nc.tensor.matmul(ps[:, XBANK, c * P:(c + 1) * P], oT[p][:, i * P:(i + 1) * P],
                                            mix[:, m0, :], start=True, stop=True)
                last.then_inc(x_ready, 1)

            for m in range(S_AHEAD):
                if m == 0:
                    pe.wait_ge(in_q[0], 16 * Q_STACK_DMAS)
                    pe.wait_ge(in_k[0], 16 * K_STACK_DMAS)
                scores(m, m - 1 if m >= 2 else None)
                if m >= S_AHEAD - T_AHEAD:
                    transposes(m - (S_AHEAD - T_AHEAD), 0, m - (S_AHEAD - T_AHEAD) + 1)
            with pe.Fori(0, UNITS) as u:
                for j in range(STEPS):
                    m = j + S_AHEAD
                    if j % 4 >= 2:
                        products(j, u)
                    if m % 16 == 0:
                        p, later = step_of(m)[0], m // STEPS
                        pe.wait_ge(in_q[p], u * (16 * Q_STACK_DMAS) + 16 * Q_STACK_DMAS * (1 + later))
                        pe.wait_ge(in_k[p], u * (16 * K_STACK_DMAS) + 16 * K_STACK_DMAS * (1 + later))
                    scores(m, u * STEPS + m - 1)
                    transposes(j + T_AHEAD, u, u * STEPS + j + T_AHEAD + 1)
                    if j == 0:
                        pe.wait_ge(o_free, u * 16 + 1)
                    for idx, (at, kind, arg) in enumerate(BANK_USES):
                        if at != j:
                            continue
                        use = u * USES + 8 + idx
                        if kind == "R":
                            rotary_product(u + 1, arg, use)
                        elif arg[0]:
                            project(1, arg[1], (u + QUADS - 1) % QUADS * 2 + 1, use)
                        else:
                            if arg[1] == 0:
                                pe.wait_ge(o_free, u * 16 + 9)
                            project(0, arg[1], u % QUADS * 2, use)
            pe.wait_ge(o_free, 16 * UNITS + 1)
            for half in range(2):
                project(1, half, 2 * QUADS - 1, UNITS * USES + 8 + half)

        @block.scalar
        def _(act):
            def copy(dst, src, scale=1.0):
                return nc.scalar.activation(dst, src, ACT.Copy, scale=scale)

            def copied(ins):
                ins.then_inc(first_act, 1)

            def bank4(bank):
                return ps[:, bank, :].rearrange("p (c n) -> p c n", c=4)

            act.wait_ge(ln_var, 1)
            nc.scalar.activation(std[:, 1, :], std[:, 0, :], ACT.Sqrt).then_inc(ln_std, 1)
            act.wait_ge(first_pe, 1)
            copy(wdT[:], ps[:, 0, 0:P])
            copied(copy(gateT[:], ps[:, 0, P:P + E]))
            for half in range(2):
                act.wait_ge(first_pe, 2 + half)
                copied(copy(wqT[:, 4 * half:4 * half + 4, :], bank4(1 + half), HD ** -0.5))
            for half in range(2):
                act.wait_ge(first_pe, 4 + half)
                copied(copy(wkT[:, 4 * half:4 * half + 4, 0, :], bank4(3 + half)))
            for half in range(2):
                act.wait_ge(first_pe, 6 + half)
                copied(copy(woT[:, 4 * half:4 * half + 4, :], bank4(5 + half)))
            for b in range(4):
                act.wait_ge(first_pe, 8 + b)
                copied(copy(xT[:, b * TB:(b + 1) * TB], ps[:, b, :]))
            for c, bank in enumerate((4, 5, 6, 0)):
                act.wait_ge(first_pe, 12 + c)
                copied(copy(lT[:, c * TB:(c + 1) * TB], ps[:, bank, :]))
            for half in range(2):
                act.wait_ge(first_pe, 17 + half)
                copied(copy(lat[:, QB * half:QB * half + QB, :],
                            ps[:, 2 + half, :].rearrange("p (i l) -> p i l", l=LAT)))
            for half in range(2):
                act.wait_ge(first_pe, 19 + half)
                copied(copy(mix[:, 4 * half:4 * half + 4, :], bank4(4 + half)))
            copied(nc.scalar.activation(route[:, 0, :], ps[:, 1, 0:TILES * E], ACT.Exp, scale=-1.0))

            def high(s):
                t, ck = s // 2, s % 2
                cols = slice(ck * TB, ck * TB + TB)
                return copy(roped[:, t, 0, :, cols], turned[:, s % 2, :, :])

            for s in range(4):
                act.wait_ge(turned_ready, s + 1)
                high(s).then_inc(hi_ready, 1)

            with act.Fori(0, B * S // TB) as tb:
                for c in range(CH):
                    act.wait_ge(up_pe, tb * CH + c + 1)
                    nc.scalar.activation(hid[:, c, :], ps[:, c % 2, :], ACT.Silu).then_inc(silu_act, 1)

            def softmax_exp(m, count):
                width = (step_of(m)[1] + 1) * P
                act.wait_ge(max_ready, count)
                nc.scalar.activation(probs[:, m % 4, 0:width], sco[m % 2][:, 0:width], ACT.Exp,
                                     bias=negmax[:, m % 4:m % 4 + 1],
                                     accum_out=den[:, m % 4:m % 4 + 1]).then_inc(exp_done, 1)

            def copy_first(m, count):
                width = min(4, step_of(m)[1] + 1) * P
                act.wait_ge(pt_ready, count)
                bank = PT0 + chunks_before(m) % 2
                copy(probsT[:, m % 2, m % 4 // 2, 0:width], ps[:, bank, 0:width]).then_inc(copied_act, 1)

            act.wait_ge(down_added, B * S // TB)
            act.sem_inc(o_free)
            for m in range(S_AHEAD):
                softmax_exp(m, m + 1)
                if m >= S_AHEAD - T_AHEAD:
                    t = m - (S_AHEAD - T_AHEAD)
                    copy_first(t, chunks_before(t) + 1)
            with act.Fori(0, UNITS) as u:
                for j in range(STEPS):
                    if j % 4 >= 2:
                        p, i, _ = step_of(j)
                        act.wait_ge(pv_done, u * 16 + j // 4 * 2 + j % 2 + 1)
                        copy(oT[p][:, i * P:(i + 1) * P], ps[:, OBANK, 0:P]).then_inc(o_free, 1)
                    if j % 2 == 0:
                        softmax_exp(j + S_AHEAD, u * STEPS + j + S_AHEAD + 1)
                    copy_first(j + T_AHEAD, u * CHUNKS + chunks_before(j + T_AHEAD) + 1)
                    if j % 2:
                        softmax_exp(j + S_AHEAD, u * STEPS + j + S_AHEAD + 1)
                    for s in range(4):
                        if HI_AT[s] == j:
                            act.wait_ge(turned_ready, u * 4 + 4 + s + 1)
                            if s == 0:
                                act.wait_ge(in_q[1], u * (16 * Q_STACK_DMAS) + 16 * Q_STACK_DMAS)
                                act.wait_ge(in_k[1], u * (16 * K_STACK_DMAS) + 16 * K_STACK_DMAS)
                            high(s).then_inc(hi_ready, 1)

        @block.vector
        def _(dve):
            own = [0]

            def then(ins):
                own[0] += 1
                ins.then_inc(dve_own, 1)
                dve.wait_ge(dve_own, own[0])

            dve.wait_ge(in_x, 16)
            for i in range(TILES):
                last = nc.vector.bn_stats(stats[:, i, :], acc[:, i, :])
            then(last)
            for i in range(TILES):
                last = nc.vector.bn_aggr(mv[:, i, :], stats[:, i, :])
            then(last)
            nc.vector.tensor_scalar(std[:, 0, :], mv[:, :, 1], EPS, None, ALU.add).then_inc(ln_var, 1)
            dve.wait_ge(ln_std, 1)
            then(nc.vector.reciprocal(std[:, 2, :], std[:, 1, :]))
            then(nc.vector.tensor_tensor(std[:, 3, :], std[:, 0, :], std[:, 2, :], ALU.mult))
            then(nc.vector.tensor_tensor(std[:, 2, :], std[:, 1, :], std[:, 3, :], ALU.add))
            then(nc.vector.tensor_scalar(std[:, 3, :], std[:, 2, :], 0.5, None, ALU.mult))
            then(nc.vector.reciprocal(std[:, 0, :], std[:, 3, :]))
            for i in range(TILES):
                nc.vector.tensor_scalar(xn[:, i, :], acc[:, i, :], mv[:, i, 0:1], std[:, 0, i:i + 1],
                                        ALU.subtract, ALU.mult).then_inc(ln_done, 1)
            for half in range(2):
                dve.wait_ge(first_act, 4 + half)
                lo = wkT[:, 4 * half:4 * half + 4, 1, :]
                hi = wkT[:, 4 * half:4 * half + 4, 0, :].bitcast(f32)
                nc.vector.tensor_tensor(lo, ps[:, 3 + half, :].rearrange("p (c n) -> p c n", c=4), hi,
                                        ALU.subtract).then_inc(first_dve, 1)
            dve.wait_ge(in_consts, 16 * 4)
            nc.vector.tensor_copy(identb[:], ident[:]).then_inc(consts_cast, 1)
            nc.vector.tensor_copy(maskb[:], mask_raw[:]).then_inc(consts_cast, 1)
            nc.vector.tensor_copy(sel[:].rearrange("p c n -> p (c n)"), sel_raw[:]).then_inc(consts_cast, 1)
            for c, bank in enumerate((4, 5, 6, 0)):
                dve.wait_ge(first_act, 12 + c)
                rows, cols = slice(LAT, 2 * LAT), slice(c * TB, (c + 1) * TB)
                nc.vector.tensor_tensor(lT[rows, cols], ps[rows, bank, :], lT[rows, cols].bitcast(f32),
                                        ALU.subtract).then_inc(first_dve, 1)

            cos, sin = rope[:, 0, :], rope[:, 1, :]

            def turn(r):
                s, t = r // 2, r % 2
                ck = s % 2
                cols = slice(ck * TB, ck * TB + TB)
                src = ps[:, XBANK, :]
                nc.vector.tensor_tensor(prod[:, s % 2, 2 * t + 0, :], src, (sin if t else cos)[:, cols], ALU.mult)
                return nc.vector.tensor_tensor(prod[:, s % 2, 2 * t + 1, :], src, (cos if t else sin)[:, cols],
                                               ALU.mult)

            def low(s):
                t, ck = s // 2, s % 2
                cols = slice(ck * TB, ck * TB + TB)
                return nc.vector.tensor_tensor(roped[:, t, 1, :, cols], turned[:, s % 2, :, :],
                                               roped[:, t, 0, :, cols].bitcast(f32), ALU.subtract)

            def turn_done(ins, r):
                ins.then_inc(x_free, 1)

            dve.wait_ge(in_rope, 16)
            for s in range(4):
                if s >= 2:
                    dve.wait_ge(hi_ready, s - 1)
                    low(s - 2).then_inc(lo_ready, 1)
                for t in range(2):
                    dve.wait_ge(x_ready, 2 * s + t + 1)
                    turn(2 * s + t).then_inc(x_free, 1)
            for s in (2, 3):
                dve.wait_ge(hi_ready, s + 1)
                low(s).then_inc(lo_ready, 1)

            dve.wait_ge(first_act, FIRST_ACT)
            G = TILES * GROUPS
            r_ = [route[:, n, :] for n in range(8)]
            then(nc.vector.tensor_scalar(r_[1], r_[0], 1.0, None, ALU.add))
            then(nc.vector.reciprocal(r_[2], r_[1]))
            four = r_[2].rearrange("p (g a b) -> p g a b", a=2, b=2)
            big, small = r_[3][:, 0:2 * G], r_[3][:, 2 * G:4 * G]
            nc.vector.tensor_tensor(big.rearrange("p (g a) -> p g a", a=2), four[:, :, :, 0], four[:, :, :, 1], ALU.max)
            then(nc.vector.tensor_tensor(small.rearrange("p (g a) -> p g a", a=2), four[:, :, :, 0], four[:, :, :, 1],
                                         ALU.min))
            b2, s2 = big.rearrange("p (g a) -> p g a", a=2), small.rearrange("p (g a) -> p g a", a=2)
            first, a1, a2, second = (r_[4][:, n * G:(n + 1) * G] for n in range(4))
            nc.vector.tensor_tensor(first, b2[:, :, 0], b2[:, :, 1], ALU.max)
            nc.vector.tensor_tensor(a1, b2[:, :, 0], b2[:, :, 1], ALU.min)
            then(nc.vector.tensor_tensor(a2, s2[:, :, 0], s2[:, :, 1], ALU.max))
            then(nc.vector.tensor_tensor(second, a1, a2, ALU.max))
            gsum, grank, gmask = (r_[5][:, n * G:(n + 1) * G] for n in range(3))
            then(nc.vector.tensor_tensor(gsum, first, second, ALU.add))

            def ranks(vals, n, over, ties, low_n, result):
                v = vals.rearrange("p (t e) -> p t e", e=n)
                other = v.unsqueeze(2).broadcast_to([P, TILES, n, n])
                this = v.unsqueeze(3).broadcast_to([P, TILES, n, n])
                nc.vector.tensor_tensor(over, other, this, ALU.is_gt)
                then(nc.vector.tensor_tensor(ties, other, this, ALU.is_equal))
                then(nc.vector.tensor_tensor(ties, ties, low_n.unsqueeze(1).broadcast_to([P, TILES, n, n]), ALU.mult))
                then(nc.vector.tensor_tensor(over, over, ties, ALU.add))
                then(nc.vector.tensor_reduce(result.rearrange("p (t e) -> p t e", e=n), over, AX.X, ALU.add))

            lower4 = lower[:, 0:GROUPS, 0:GROUPS]
            cmp4 = [r_[n].rearrange("p (t a b) -> p t a b", a=GROUPS, b=GROUPS) for n in (6, 7)]
            dve.wait_ge(in_consts, 16 * 4)
            ranks(gsum, GROUPS, cmp4[0], cmp4[1], lower4, grank)
            then(nc.vector.tensor_scalar(gmask, grank, float(TOPG), None, ALU.is_lt))
            masked = r_[1]
            then(nc.vector.tensor_tensor(masked.rearrange("p (g e) -> p g e", e=E // GROUPS),
                                         r_[2].rearrange("p (g e) -> p g e", e=E // GROUPS),
                                         gmask.unsqueeze(2).broadcast_to([P, G, E // GROUPS]), ALU.mult))
            wide = hid[:].rearrange("p c n -> p (c n)")[:, 0:TILES * E * E].bitcast(bf16)
            cmp16 = [wide[:, n * TILES * E * E:(n + 1) * TILES * E * E]
                     .rearrange("p (t a b) -> p t a b", a=E, b=E) for n in range(2)]
            ranks(masked, E, cmp16[0], cmp16[1], lower[:], r_[3])
            then(nc.vector.tensor_scalar(r_[4], r_[3], float(TOPK), None, ALU.is_lt))
            then(nc.vector.tensor_tensor(r_[5], r_[2], r_[4], ALU.mult))
            chosen = r_[5].rearrange("p (t e) -> p t e", e=E)
            then(nc.vector.tensor_reduce(r_[6][:, 0:TILES], chosen, AX.X, ALU.add))
            then(nc.vector.tensor_scalar(r_[6][:, TILES:2 * TILES], r_[6][:, 0:TILES], 1e-20, None, ALU.add))
            then(nc.vector.reciprocal(r_[6][:, 0:TILES], r_[6][:, TILES:2 * TILES]))
            then(nc.vector.tensor_tensor(r_[7].rearrange("p (t e) -> p t e", e=E), chosen,
                                         r_[6][:, 0:TILES].unsqueeze(2).broadcast_to([P, TILES, E]), ALU.mult))
            then(nc.vector.tensor_scalar(r_[0], r_[7], SCALING, None, ALU.mult))
            dve.wait_ge(zeroed, 1)
            rest = r_[0]
            for part in range(3):
                to = comb3[:, :, 32 * part:32 * part + E]
                left = rest.rearrange("p (t e) -> p t e", e=E)
                if part == 2:
                    nc.vector.tensor_copy(to, left).then_inc(comb_done, 1)
                else:
                    then(nc.vector.tensor_copy(to, left))
                    nxt = r_[1 + part]
                    then(nc.vector.tensor_tensor(nxt.rearrange("p (t e) -> p t e", e=E), left, to, ALU.subtract))
                    rest = nxt
            dve.wait_ge(combT_pe, 1)
            for half in range(2):
                ins = nc.vector.tensor_copy(cT[:, half * S:(half + 1) * S], ps[:, 5 + half, :].bitcast(bf16))
            ins.then_inc(combT_done, 1)
            with dve.Fori(0, B * S // TB) as tb:
                for c in range(ECH):
                    dve.wait_ge(silu_act, tb * CH + c + 1)
                    nc.vector.tensor_tensor(hid[:, c, :], hid[:, c, :], ps[:, 2 + c % 2, :],
                                            ALU.mult).then_inc(gated, 1)
                dve.wait_ge(down_pe, tb + 1)
                rows = acc[:, bass.ds(tb * 4, 4), :]
                nc.vector.tensor_tensor(rows, rows, ps[:, 4, :].rearrange("p (c n) -> p c n", c=4),
                                        ALU.add).then_inc(down_added, 1)
            def row_max(m, count):
                width = (step_of(m)[1] + 1) * P
                dve.wait_ge(s_ready, count)
                nc.vector.tensor_reduce(negmax[:, m % 4:m % 4 + 1], sco[m % 2][:, 0:width], AX.X, ALU.max,
                                        negate=True).then_inc(max_ready, 1)

            def row_rden(m, count):
                dve.wait_ge(exp_done, count)
                nc.vector.reciprocal(rden[:, m % 4:m % 4 + 1], den[:, m % 4:m % 4 + 1]).then_inc(rden_ready, 1)

            def copy_second(m, count):
                width = (step_of(m)[1] + 1 - 4) * P
                bank = PT0 + (chunks_before(m) + 1) % 2
                dve.wait_ge(pt_ready, count)
                nc.vector.tensor_copy(probsT[:, m % 2, m % 4 // 2, TB:TB + width],
                                      ps[:, bank, 0:width]).then_inc(copied_dve, 1)

            def add_projected(use, tile0):
                dve.wait_ge(x_ready, use)
                rows = acc[:, bass.ds(tile0, 4), :]
                nc.vector.tensor_tensor(rows, rows, ps[:, XBANK, :].rearrange("p (c n) -> p c n", c=4),
                                        ALU.add).then_inc(x_free, 1)

            for m in range(S_AHEAD):
                row_max(m, m + 1)
                if m >= 1:
                    row_rden(m - 1, m)
                if m >= S_AHEAD - T_AHEAD:
                    t = m - (S_AHEAD - T_AHEAD)
                    if chunks_of(t) == 2:
                        copy_second(t, chunks_before(t) + 2)
            with dve.Fori(0, UNITS) as u:
                for j in range(STEPS):
                    if j % 2:
                        row_rden(j + S_AHEAD - 1, u * STEPS + j + S_AHEAD)
                    row_max(j + S_AHEAD, u * STEPS + j + S_AHEAD + 1)
                    if j % 2 == 0:
                        row_rden(j + S_AHEAD - 1, u * STEPS + j + S_AHEAD)
                    if chunks_of(j + T_AHEAD) == 2:
                        copy_second(j + T_AHEAD, u * CHUNKS + chunks_before(j + T_AHEAD) + 2)
                    for idx, (at, kind, arg) in enumerate(BANK_USES):
                        if at != j:
                            continue
                        use = u * USES + 8 + idx + 1
                        if kind == "R":
                            dve.wait_ge(x_ready, use)
                            turn(arg).then_inc(x_free, 1)
                        elif arg[0]:
                            add_projected(use, u // (QUADS + 1) * QB + 4 * arg[1])
                        else:
                            add_projected(use, u // QUADS * QB + 4 * arg[1])
                    for s in range(4):
                        if LO_AT[s] == j:
                            dve.wait_ge(hi_ready, u * 4 + 4 + s + 1)
                            low(s).then_inc(lo_ready, 1)
            for half in range(2):
                add_projected(UNITS * USES + 8 + half + 1, (B - 1) * QB + 4 * half)

        @block.gpsimd
        def _(pool):
            nc.gpsimd.memset(comb3[:], 0.0).then_inc(zeroed, 1)

            def rotate_a(s):
                return nc.gpsimd.tensor_tensor(turned[:, s % 2, 0, :], prod[:, s % 2, 0, :], prod[:, s % 2, 2, :],
                                               ALU.subtract)

            def rotate_b(s):
                return nc.gpsimd.tensor_tensor(turned[:, s % 2, 1, :], prod[:, s % 2, 3, :], prod[:, s % 2, 1, :],
                                               ALU.add)

            for s in range(4):
                pool.wait_ge(x_free, 2 * s + 2)
                if s >= 2:
                    pool.wait_ge(lo_ready, s - 1)
                rotate_a(s)
                rotate_b(s).then_inc(turned_ready, 1)

            def divide(m, count):
                width = (step_of(m)[1] + 1) * P
                pool.wait_ge(rden_ready, count)
                pool.sem_inc(divide_begun)
                row = probs[:, m % 4, 0:width]
                nc.gpsimd.tensor_scalar(row, row, rden[:, m % 4:m % 4 + 1], 1.0, ALU.mult, ALU.mult)\
                    .then_inc(p_ready, 1)

            pool.wait_ge(combT_pe, 1)
            nc.gpsimd.memset(oT[1][:], 0.0).then_inc(zeroed, 1)
            for m in range(S_AHEAD - 1):
                divide(m, m + 1)
            with pool.Fori(0, UNITS) as u:
                for j in range(STEPS):
                    divide(j + S_AHEAD - 1, u * STEPS + j + S_AHEAD)
                    for s in range(4):
                        if ADD_AT[s][0] == j:
                            upto = [i for i, (_, kind, arg) in enumerate(BANK_USES) if kind == "R" and arg == 2 * s + 1]
                            pool.wait_ge(x_free, u * USES + 8 + upto[0] + 1)
                            rotate_a(s)
                        if ADD_AT[s][1] == j:
                            rotate_b(s).then_inc(turned_ready, 1)


FIRST_JOBS = 20
FIRST_ACT = 20
FIRST_ACT_LAT = 17
FIRST_DVE_WK = 2


def copier_of(k):
    unit, k = k // CHUNKS, k % CHUNKS
    m = n = 0
    while n + chunks_of(m) <= k:
        n += chunks_of(m)
        m += 1
    if k - n:
        return 1, unit * SECONDS + seconds_before(m) + 1, SECONDS
    return 0, unit * STEPS + m + 1, STEPS


def kernel(L0_attn_x, L0_attn_wq, L0_attn_w_kv_down, L0_attn_w_k_up, L0_attn_w_v_up, L0_attn_wo,
           L0_ffn_gate_weight, L0_ffn_expert_up, L0_ffn_expert_down, L0_ffn_shared_up, L0_ffn_shared_down):
    import concourse.bacc as bacc
    from concourse.bass_utils import run_bass_kernel_spmd

    inv_freq = (np.float32(1.0) / np.float32(10000.0) ** (np.arange(0, HD, 2, dtype=np.float32) / np.float32(HD)))
    angle = (np.arange(S, dtype=np.float32)[None, :] * inv_freq[:, None]).astype(np.float32)
    rope = np.stack([np.cos(angle), np.sin(angle)], 1).astype(np.float32)
    rope = np.ascontiguousarray(np.tile(rope, (4, 1, 1)))
    sel = np.zeros((P, ECH, P), np.float32)
    for part in range(3):
        for e in range(E):
            sel[32 * part + e, e // 2, EI * (e % 2):EI * (e % 2) + EI] = 1.0
    lower = np.ascontiguousarray(np.broadcast_to(np.tril(np.ones((E, E), np.float32), -1), (P, E, E)))
    arrays = {
        "x": L0_attn_x, "wq": L0_attn_wq, "w_down": L0_attn_w_kv_down, "w_kup": L0_attn_w_k_up,
        "w_vup": L0_attn_w_v_up, "wo": L0_attn_wo, "gate": L0_ffn_gate_weight, "e_up": L0_ffn_expert_up,
        "e_down": L0_ffn_expert_down, "s_up": L0_ffn_shared_up, "s_down": L0_ffn_shared_down,
        "c_rope": rope, "c_ident": np.eye(P, dtype=np.float32),
        "c_mask": np.triu(np.full((P, P), -1e30, np.float32), 1),
        "c_sel": sel.reshape(P, ECH * P), "c_lower": lower,
    }
    nc = bacc.Bacc("TRN2", target_bir_lowering=False, num_devices=1)
    args = []
    for name in list(arrays):
        a = np.ascontiguousarray(arrays[name])
        arrays[name] = a
        args.append(nc.dram_tensor(name, a.shape, mybir.dt.from_np(a.dtype), kind="ExternalInput").ap())
    args.append(nc.dram_tensor("out", (B, S, D), f32, kind="ExternalOutput").ap())
    block_kernel(nc, *args)
    r = run_bass_kernel_spmd(nc, [arrays], core_ids=[0])
    return r.results[0]["out"]
```

```python
from contextlib import ExitStack

import numpy as np

import concourse.bass as bass
from concourse import mybir

f32 = mybir.dt.float32
f32r = mybir.dt.float32r
bf16 = mybir.dt.bfloat16
ALU = mybir.AluOpType
ACT = mybir.ActivationFunctionType
AX = mybir.AxisListType

P = 128
B, S, D = 2, 1024, 128
HEADS, HD, LAT = 16, 64, 64
TILES = B * S // P
QB = S // P
QUADS = HEADS // 4
UNITS = B * QUADS
HALF = HD // 2
E, EI, SI = 16, 64, 256
CH = (E * EI + SI) // P
ECH = E * EI // P
GROUPS, TOPG, TOPK = 4, 2, 4
SCALING = 2.5
EPS = 1e-5
TB = 512

LONG, SHORT = [7, 6, 5, 4], [0, 1, 2, 3]
STEPS = 4 * QB
S_AHEAD, T_AHEAD = 5, 2


def step_of(m):
    m %= STEPS
    return m // (2 * QB), (SHORT if m % 2 else LONG)[m % (2 * QB) // 4], m % 4 // 2


def chunks_of(m):
    return 2 if step_of(m)[1] >= 4 else 1


CHUNKS = sum(chunks_of(m) for m in range(STEPS))
SECONDS = sum(chunks_of(m) - 1 for m in range(STEPS))


def chunks_before(m):
    return m // STEPS * CHUNKS + sum(chunks_of(n) for n in range(m % STEPS))


def seconds_before(m):
    return m // STEPS * SECONDS + sum(chunks_of(n) - 1 for n in range(m % STEPS))


def gated_upto(k):
    return k // CH * ECH + min(k % CH + 1, ECH)


def half_of(s):
    return slice(s % 2 * TB, s % 2 * TB + TB)


BANK_USES = [(0, "R", 0), (1, "R", 1), (3, "R", 2), (4, "R", 3), (6, "R", 4), (7, "R", 5), (9, "R", 6), (10, "R", 7),
             (12, "O", (1, 0)), (14, "O", (1, 1)), (18, "O", (0, 0)), (20, "O", (0, 1))]
USES = len(BANK_USES)
ADD_AT, HI_AT, LO_AT = [(2, 3), (5, 6), (8, 9), (11, 12)], [4, 7, 10, 13], [5, 8, 11, 14]
PAD = E // 2
PASSES, PASS_CH, DOWN_LAG = B * S // (2 * TB), 2 * CH, 2
EARLY_ROTARY = [(0, 0), (2, 1), (5, 4), (8, 5)]
Q_STACK_DMAS, K_STACK_DMAS = 2 * 4, 2 * 8


def block_kernel(nc, x, wq, w_down, w_kup, w_vup, wo, gate, e_up, e_down, s_up, s_down,
                 c_rope, c_ident, c_mask, c_sel, c_lower, out):
    ctx = ExitStack()
    with ctx:
        def sb(name, shape, dt, into=ctx):
            return into.enter_context(nc.sbuf_tensor(name, shape, dt))

        def sem(name):
            return ctx.enter_context(nc.semaphore(name))

        acc = sb("acc", [P, TILES, P], f32)
        rope = sb("rope", [P, 2, S], f32)
        xT = sb("xT", [P, B * S], f32)
        lT = sb("lT", [P, B * S], f32r)
        wqT = sb("wqT", [P, 2 * QUADS, P], f32)
        wkT = sb("wkT", [P, 2 * QUADS, 2, P], f32r)
        wq_now = sb("wq_now", [P, 2, P], f32)
        wk_now = sb("wk_now", [P, 2, 2, P], f32r)
        lat = sb("lat", [P, TILES, LAT], f32)
        lat_now = [sb(f"lat_now{p}", [P, QB, LAT], f32) for p in range(2)]
        mix = sb("mix", [P, HEADS // 2, P], f32)
        ident = sb("ident", [P, P], f32)
        identb = sb("identb", [P, P], bf16)
        maskb = sb("maskb", [P, P], bf16)
        roped = sb("roped", [P, 2, 2, 2, S], f32r)
        prod = sb("prod", [P, 2, 4, TB], f32)
        turned = sb("turned", [P, 2, 2, TB], f32)
        negmax = sb("negmax", [P, 4], f32)
        den = sb("den", [P, 4], f32)
        rden = sb("rden", [P, 4], f32)

        early = ExitStack()
        with early:
            hid = sb("hid", [P, CH, TB], f32, early)
            up = sb("up", [P, CH * P], f32, early)
            down = sb("down", [P, CH, P], f32, early)
            sel = sb("sel", [P, ECH, P], bf16, early)
            cT = sb("cT", [P, B * S], bf16, early)
            xn = sb("xn", [P, TILES, P], f32, early)
            top8 = sb("top8", [P, TILES, 8], f32, early)
            prefix = sb("prefix", [P, 2, TILES, PAD + E], f32, early)
            wq_raw = sb("wq_raw", [P, 2 * QUADS, D], f32, early)
            wk_raw = sb("wk_raw", [P, 2 * QUADS, 2, LAT], f32, early)
            wv_raw = sb("wv_raw", [P, HEADS // 2, LAT], f32, early)
            wo_raw = sb("wo_raw", [P, HEADS // 2, P], f32, early)
            woT = sb("woT", [P, HEADS // 2, P], f32, early)
            comb3 = sb("comb3", [P, TILES, P], bf16, early)
            sel_raw = sb("sel_raw", [P, ECH * P], f32, early)
            lower = sb("lower", [P, E, E], f32, early)
            mask_raw = sb("mask_raw", [P, P], f32, early)
            gate_raw = sb("gate_raw", [E, D], f32, early)
            gateT = sb("gateT", [P, E], f32, early)
            wd_raw = sb("wd_raw", [P, D], f32, early)
            wdT = sb("wdT", [P, P], f32, early)
            stats = sb("stats", [P, TILES, 6], f32, early)
            mv = sb("mv", [P, TILES, 2], f32, early)
            std = sb("std", [P, 4, TILES], f32, early)
            route = sb("route", [P, 8, TILES * E], f32, early)
        probs = sb("probs", [P, 4, S], f32)
        probsT = sb("probsT", [P, 2, 2, S], f32)
        oT = [sb("oT0", [P, S], f32), None]
        qs = [sb(f"qs{n}", [P, S], f32r) for n in range(4)]
        kh = [sb(f"kh{n}", [P, S], f32r) for n in range(4)]
        kl = [sb(f"kl{n}", [P, S], f32r) for n in range(4)]
        oT[1] = sb("oT1", [P, S], f32)

        ps = ctx.enter_context(nc.psum_tensor("ps", [P, 8, TB], f32))
        sco = [ps[:, 0:2, :].rearrange("p a n -> p (a n)"), ps[:, 2:4, :].rearrange("p a n -> p (a n)")]
        PT0, OBANK, XBANK = 4, 6, 7

        def halves(bank, t):
            return ps[:, bank, :].rearrange("p (g h t j) -> p t g h j", g=2, h=4, t=2)[:, t]

        def quad_rows(weights, t):
            return weights.rearrange("p (g t) (h j) -> p t g h j", t=2, h=4)[:, t]

        in_ident, in_consts, in_small, in_wq, in_wk, in_wv, in_rope, in_exp = map(
            sem, "in_ident in_consts in_small in_wq in_wk in_wv in_rope in_exp".split())
        in_x = [sem("in_x0"), sem("in_x1")]
        zeroed, ln_var, ln_std, ln_done, dve_own = map(sem, "zeroed ln_var ln_std ln_done dve_own".split())
        consts_cast, first_pe, first_act, first_dve = map(sem, "consts_cast first_pe first_act first_dve".split())
        sig_exp, comb_done, combT_pe, combT_done = map(sem, "sig_exp comb_done combT_pe combT_done".split())
        up_pe, silu_act, gated, down_pe, down_added, hid_free = map(
            sem, "up_pe silu_act gated down_pe down_added hid_free".split())
        s_ready, max_ready, exp_done, rden_ready, p_ready = map(
            sem, "s_ready max_ready exp_done rden_ready p_ready".split())
        pt_ready, copied_act, copied_dve, pv_done, o_free = map(
            sem, "pt_ready copied_act copied_dve pv_done o_free".split())
        x_ready, x_free, prod_ready, turned_ready, hi_ready, lo_ready = map(
            sem, "x_ready x_free prod_ready turned_ready hi_ready lo_ready".split())
        in_stage, stored, divide_begun = sem("in_stage"), sem("stored"), sem("divide_begun")
        in_lat = [sem("in_lat0"), sem("in_lat1")]
        in_q = [sem("in_q0"), sem("in_q1")]
        in_k = [sem("in_k0"), sem("in_k1")]

        block = ctx.enter_context(nc.Block())

        @block.sync
        def _(sp):
            x_tiles = x.rearrange("b (i p) d -> p (b i) d", p=P)
            for half in range(2):
                tiles = slice(QB * half, QB * half + QB)
                sp.dma_start(acc[:, tiles, :], x_tiles[:, tiles, :]).then_inc(in_x[half], 16)
            for twice in range(2):
                sp.dma_start(wk_raw[:, :, twice, :], w_kup.rearrange("(c p) l -> p c l", p=P)).then_inc(in_wk, 16)
            sp.dma_start(lower[:], c_lower).then_inc(in_consts, 16)
            sp.dma_start(mask_raw[:], c_mask).then_inc(in_consts, 16)
            sp.dma_start(sel_raw[:], c_sel).then_inc(in_consts, 16)
            sp.dma_start(down[:, 0:ECH, :], e_down.rearrange("(c f) i h -> (f i) c h", f=2)).then_inc(in_exp, 16)
            sp.dma_start(down[:, ECH:, :], s_down.rearrange("(c p) h -> p c h", p=P)).then_inc(in_exp, 16)

            def stage_weights(n):
                g = n % QUADS
                sp.dma_start(wq_now[:], wqT[:, bass.ds(2 * g, 2), :]).then_inc(in_stage, 16)
                sp.dma_start(wk_now[:].bitcast(f32), wkT[:, bass.ds(2 * g, 2), :, :].bitcast(f32)).then_inc(in_stage, 16)

            def stage_latent(n, p):
                b = (n // QUADS) % B
                sp.dma_start(lat_now[p][:], lat[:, bass.ds(QB * b, QB), :]).then_inc(in_lat[p], 16)

            def stack_q(p):
                for a in range(2):
                    src = roped[HALF * (2 * p + a):HALF * (2 * p + a) + HALF, 0]
                    for h in range(2):
                        for t in range(2):
                            at = HD * h + HALF * t
                            sp.dma_start(qs[2 * p + a][at:at + HALF, :].bitcast(f32),
                                         src[:, h, t, :].bitcast(f32)).then_inc(in_q[p], 16)

            def stack_k(p):
                for a in range(2):
                    src = roped[HALF * (2 * p + a):HALF * (2 * p + a) + HALF, 1]
                    for h, dst in ((0, kh), (1, kl)):
                        for twice in range(2):
                            for t in range(2):
                                at = HD * twice + HALF * t
                                sp.dma_start(dst[2 * p + a][at:at + HALF, :].bitcast(f32),
                                             src[:, h, t, :].bitcast(f32)).then_inc(in_k[p], 16)

            sp.wait_ge(first_act, FIRST_ACT_LAT)
            sp.wait_ge(first_dve, FIRST_DVE_WK)
            stage_weights(0)
            for p in range(2):
                stage_latent(0, p)
            sp.wait_ge(x_ready, 8)
            stage_weights(1)
            sp.wait_ge(combT_pe, 1)
            sp.wait_ge(consts_cast, 3)
            sp.wait_ge(first_pe, FIRST_JOBS)
            sp.wait_ge(lo_ready, 4)
            for p in range(2):
                stack_q(p)
                stack_k(p)

            with sp.Fori(0, UNITS) as u:
                n = u + 1
                sp.wait_ge(lo_ready, u * 4 + 6)
                sp.wait_ge(s_ready, u * STEPS + 16)
                stack_q(0)
                sp.wait_ge(x_ready, u * USES + 8 + 8)
                stage_weights(n + 1)
                sp.wait_ge(pv_done, u * 16 + 8)
                stage_latent(n, 0)
                sp.wait_ge(lo_ready, u * 4 + 8)
                stack_k(0)
                sp.wait_ge(s_ready, u * STEPS + 32)
                stack_q(1)
                stack_k(1)
                sp.wait_ge(pv_done, u * 16 + 16)
                stage_latent(n, 1)

            sp.wait_ge(x_free, UNITS * USES + 8 + 2)
            sp.dma_start(out.rearrange("b (i p) d -> p (b i) d", p=P), acc[:]).then_inc(stored, 16)
            sp.wait_ge(stored, 16)

        @block.tensor
        def _(pe):
            def done(ins):
                ins.then_inc(first_pe, 1)

            pe.wait_ge(in_ident, 16)
            pe.wait_ge(in_small, 16 * 3)
            nc.tensor.transpose(ps[:, 0, 0:P], wd_raw[:], ident[:])
            done(nc.tensor.transpose(ps[:, 0, P:P + E], gate_raw[:], ident[0:E, 0:E]))
            pe.wait_ge(in_wq, 16)
            for half in range(2):
                for c in range(4):
                    last = nc.tensor.transpose(ps[:, 1 + half, c * P:(c + 1) * P], wq_raw[:, 4 * half + c, :], ident[:])
                done(last)
            pe.wait_ge(in_wk, 16 * 2)
            for half in range(2):
                for c in range(4):
                    last = nc.tensor.transpose(ps[:, 3 + half, c * P:(c + 1) * P],
                                               wk_raw[:, 4 * half + c, :, :].rearrange("p a l -> p (a l)"), ident[:])
                done(last)
            pe.wait_ge(in_wv, 16 * 2)
            for half in range(2):
                for c in range(4):
                    last = nc.tensor.transpose(ps[:, 5 + half, c * P:(c + 1) * P], wo_raw[:, 4 * half + c, :], ident[:])
                done(last)
            for b, bank in enumerate((7, 0, 1, 2)):
                pe.wait_ge(ln_done, 4 * (b + 1))
                if b:
                    pe.wait_ge(first_act, b)
                for c in range(4):
                    last = nc.tensor.transpose(ps[:, bank, c * P:(c + 1) * P], xn[:, 4 * b + c, :], ident[:])
                done(last)
            pe.wait_ge(first_act, 11)
            pe.wait_ge(first_dve, 1)
            for i in range(TILES):
                last = nc.tensor.matmul(ps[:, 3, i * E:(i + 1) * E], xT[:, i * P:(i + 1) * P], gateT[:],
                                        start=True, stop=True)
            done(last)
            pe.wait_ge(first_dve, 2)
            for c in range(4):
                done(nc.tensor.matmul(ps[:, 4 + c, :], wdT[:], xT[:, c * TB:(c + 1) * TB], start=True, stop=True))
            for half in range(2):
                for i in range(QB):
                    last = nc.tensor.matmul(ps[:, half, i * LAT:(i + 1) * LAT],
                                            xT[:, (QB * half + i) * P:(QB * half + i + 1) * P], wdT[:, 0:LAT],
                                            start=True, stop=True)
                done(last)
            for half in range(2):
                if half:
                    pe.wait_ge(first_act, 12)
                for c in range(4):
                    for a in range(2):
                        rows = slice(HD * a, HD * a + HD)
                        last = nc.tensor.matmul(ps[rows, 2 + half, c * P:(c + 1) * P], wv_raw[rows, 4 * half + c, :],
                                                woT[rows, 4 * half + c, :], start=True, stop=True)
                done(last)

            def rotary_product(r, cols):
                t = r % 2
                if r < 4:
                    last = nc.tensor.matmul(ps[:, XBANK, :], wq_now[:, t, :], xT[:, cols], start=True, stop=True)
                else:
                    nc.tensor.matmul(ps[:, XBANK, :], wk_now[:, t, 0, :], lT[:, cols], start=True, stop=False)
                    last = nc.tensor.matmul(ps[:, XBANK, :], wk_now[:, t, 1, :], lT[:, cols], start=False, stop=True)
                last.then_inc(x_ready, 1)

            pe.wait_ge(first_act, 20)
            pe.wait_ge(first_dve, 6)
            pe.wait_ge(consts_cast, 3)
            pe.wait_ge(in_exp, 64)
            pe.wait_ge(in_stage, 32)
            pe.wait_ge(comb_done, 1)
            for i in range(TILES):
                bank = ps[:, 2 + i // 8, :].bitcast(bf16)
                last = nc.tensor.transpose(bank[:, i % 8 * P:(i % 8 + 1) * P], comb3[:, i, :], identb[:])
            last.then_inc(combT_pe, 1)
            pe.wait_ge(combT_done, 1)
            with pe.Fori(0, PASSES) as w:
                for k in range(PASS_CH + DOWN_LAG):
                    if k < PASS_CH:
                        c = k % CH
                        cols = bass.ds(w * (2 * TB) + k // CH * TB, TB)
                        if k >= 2:
                            if (k - 2) % CH < ECH:
                                pe.wait_ge(gated, w * (2 * ECH) + gated_upto(k - 2))
                            else:
                                pe.wait_ge(silu_act, w * PASS_CH + k - 1)
                        last = nc.tensor.matmul(ps[:, k % 2, :], up[:, c * P:(c + 1) * P], xT[:, cols],
                                                start=True, stop=True)
                        if c < ECH:
                            last = nc.tensor.matmul(ps[:, 2 + k % 2, :], sel[:, c, :], cT[:, cols],
                                                    start=True, stop=True)
                        last.then_inc(up_pe, 1)
                    for r_at, r in EARLY_ROTARY:
                        if r_at == k:
                            if r != EARLY_ROTARY[0][1]:
                                pe.wait_ge(x_free, w * 4 + EARLY_ROTARY.index((r_at, r)))
                            rotary_product(r, bass.ds(w * TB, TB))
                    d = k - DOWN_LAG
                    if d >= 0:
                        c = d % CH
                        if c < ECH:
                            pe.wait_ge(gated, w * (2 * ECH) + gated_upto(d))
                        else:
                            pe.wait_ge(silu_act, w * PASS_CH + d + 1)
                        for i in range(TB // P):
                            last = nc.tensor.matmul(ps[:, 4 + d // CH, i * P:(i + 1) * P],
                                                    hid[:, c, i * P:(i + 1) * P], down[:, c, :],
                                                    start=(c == 0 and i == 0), stop=(c == CH - 1 and i == TB // P - 1))
                        last.then_inc(down_pe, 1)
                pe.wait_ge(x_free, w * 4 + 4)
                pe.wait_ge(down_added, w * 2 + 2)

            def scores(m, count):
                p, i, a = step_of(m)
                if m == 0 or m >= 2:
                    if count is not None:
                        pe.wait_ge(exp_done, count)
                n, width = 2 * p + a, (i + 1) * P
                q = qs[n][:, i * P:(i + 1) * P]
                out_ps = sco[m % 2]
                for lo in range(0, width, TB):
                    hi = min(lo + TB, max(width, lo + 2 * P))
                    nc.tensor.matmul(out_ps[:, lo:hi], q, kh[n][:, lo:hi], start=True, stop=False)
                    if lo <= i * P < hi:
                        nc.tensor.matmul(out_ps[:, i * P:(i + 1) * P], identb[:], maskb[:], start=False, stop=False)
                    last = nc.tensor.matmul(out_ps[:, lo:hi], q, kl[n][:, lo:hi], start=False, stop=True)
                last.then_inc(s_ready, 1)

            def transposes(m, u, probs_count):
                _, i, _ = step_of(m)
                pe.wait_ge(p_ready, probs_count)
                for x_ in range(chunks_of(m)):
                    k = chunks_before(m) + x_ - 2
                    if k >= 0:
                        by, base, per = copier_of(k)
                        pe.wait_ge(copied_dve if by else copied_act, u * per + base)
                    for kb in range(4 * x_, min(4 * x_ + 4, i + 1)):
                        bank = PT0 + (chunks_before(m) + x_) % 2
                        last = nc.tensor.transpose(ps[:, bank, kb % 4 * P:(kb % 4 + 1) * P],
                                                   probs[:, m % 4, kb * P:(kb + 1) * P], ident[:])
                    last.then_inc(pt_ready, 1)

            def products(m, u):
                p, i, _ = step_of(m)
                k = m // 4 * 2 + m % 2
                if k % 8 == 0:
                    pe.wait_ge(in_lat[p], u * 16 + 16)
                pe.wait_ge(o_free, u * 16 + k + 1)
                pe.wait_ge(copied_act, u * STEPS + m + 1)
                pe.wait_ge(copied_dve, u * SECONDS + seconds_before(m + 1))
                for kb in range(i + 1):
                    for a in range(2):
                        last = nc.tensor.matmul(ps[HD * a:HD * a + HD, OBANK, 0:P], lat_now[p][:, kb, :],
                                                probsT[:, m % 2, a, kb * P:(kb + 1) * P],
                                                start=(kb == 0), stop=(kb == i))
                last.then_inc(pv_done, 1)

            def project(p, half, m0, use):
                pe.wait_ge(x_free, use)
                for c in range(4):
                    i = 4 * half + c
                    last = nc.tensor.matmul(ps[:, XBANK, c * P:(c + 1) * P], oT[p][:, i * P:(i + 1) * P],
                                            mix[:, m0, :], start=True, stop=True)
                last.then_inc(x_ready, 1)

            for m in range(S_AHEAD):
                if m == 0:
                    pe.wait_ge(in_q[0], 16 * Q_STACK_DMAS)
                    pe.wait_ge(in_k[0], 16 * K_STACK_DMAS)
                scores(m, m - 1 if m >= 2 else None)
                if m >= S_AHEAD - T_AHEAD:
                    transposes(m - (S_AHEAD - T_AHEAD), 0, m - (S_AHEAD - T_AHEAD) + 1)
            with pe.Fori(0, UNITS) as u:
                for j in range(STEPS):
                    m = j + S_AHEAD
                    if j % 4 >= 2:
                        products(j, u)
                    if m % 16 == 0:
                        p, later = step_of(m)[0], m // STEPS
                        pe.wait_ge(in_q[p], u * (16 * Q_STACK_DMAS) + 16 * Q_STACK_DMAS * (1 + later))
                        pe.wait_ge(in_k[p], u * (16 * K_STACK_DMAS) + 16 * K_STACK_DMAS * (1 + later))
                    scores(m, u * STEPS + m - 1)
                    transposes(j + T_AHEAD, u, u * STEPS + j + T_AHEAD + 1)
                    if j == 0:
                        pe.wait_ge(o_free, u * 16 + 1)
                    for idx, (at, kind, arg) in enumerate(BANK_USES):
                        if at != j:
                            continue
                        use = u * USES + 8 + idx
                        if kind == "R":
                            if arg == 0:
                                pe.wait_ge(in_stage, u * 32 + 64)
                            pe.wait_ge(x_free, use)
                            rotary_product(arg, bass.ds((u + 1) // QUADS % B * S + arg % 4 // 2 * TB, TB))
                        elif arg[0]:
                            project(1, arg[1], (u + QUADS - 1) % QUADS * 2 + 1, use)
                        else:
                            if arg[1] == 0:
                                pe.wait_ge(o_free, u * 16 + 9)
                            project(0, arg[1], u % QUADS * 2, use)
            pe.wait_ge(o_free, 16 * UNITS + 1)
            for half in range(2):
                project(1, half, 2 * QUADS - 1, UNITS * USES + 8 + half)

        @block.scalar
        def _(act):
            def copy(dst, src, scale=1.0):
                return nc.scalar.activation(dst, src, ACT.Copy, scale=scale)

            def copied(ins):
                ins.then_inc(first_act, 1)

            def bank4(bank):
                return ps[:, bank, :].rearrange("p (c n) -> p c n", c=4)

            act.dma_start(ident[:], c_ident).then_inc(in_ident, 16)
            for half in range(2):
                act.dma_start(wd_raw[LAT * half:LAT * half + LAT, :], w_down).then_inc(in_small, 16)
            act.dma_start(gate_raw[:], gate).then_inc(in_small, 16)
            act.dma_start(wq_raw[:], wq.rearrange("(c p) d -> p c d", p=P)).then_inc(in_wq, 16)
            act.dma_start(wo_raw[:].rearrange("p c r -> p (c r)"), wo).then_inc(in_wv, 16)
            act.dma_start(wv_raw[:], w_vup.rearrange("(c p) l -> p c l", p=P)).then_inc(in_wv, 16)
            act.dma_start(up[:, E * EI:], s_up).then_inc(in_exp, 16)
            act.dma_start(up[:, 0:E * EI].rearrange("p (e i) -> p e i", i=EI),
                          e_up.rearrange("e h i -> h e i")).then_inc(in_exp, 16)
            act.dma_start(rope[:], c_rope).then_inc(in_rope, 16)

            act.wait_ge(ln_var, 1)
            nc.scalar.activation(std[:, 1, :], std[:, 0, :], ACT.Sqrt).then_inc(ln_std, 1)
            act.wait_ge(first_pe, 1)
            copy(wdT[:], ps[:, 0, 0:P])
            copied(copy(gateT[:], ps[:, 0, P:P + E]))
            for half in range(2):
                act.wait_ge(first_pe, 2 + half)
                for t in range(2):
                    last = copy(quad_rows(wqT[:, 4 * half:4 * half + 4, :], t), halves(1 + half, t), HD ** -0.5)
                copied(last)
            for half in range(2):
                act.wait_ge(first_pe, 4 + half)
                for t in range(2):
                    last = copy(quad_rows(wkT[:, 4 * half:4 * half + 4, 0, :], t), halves(3 + half, t))
                copied(last)
            for half in range(2):
                act.wait_ge(first_pe, 6 + half)
                copied(copy(woT[:, 4 * half:4 * half + 4, :], bank4(5 + half)))
            for b, bank in enumerate((7, 0, 1, 2)):
                act.wait_ge(first_pe, 8 + b)
                copied(copy(xT[:, b * TB:(b + 1) * TB], ps[:, bank, :]))
            act.wait_ge(first_pe, 12)
            copied(nc.scalar.activation(route[:, 0, :], ps[:, 3, 0:TILES * E], ACT.Exp, scale=-1.0))
            for c in range(4):
                act.wait_ge(first_pe, 13 + c)
                copied(copy(lT[:, c * TB:(c + 1) * TB], ps[:, 4 + c, :]))
            for half in range(2):
                act.wait_ge(first_pe, 17 + half)
                copied(copy(lat[:, QB * half:QB * half + QB, :],
                            ps[:, half, :].rearrange("p (i l) -> p i l", l=LAT)))
            for half in range(2):
                act.wait_ge(first_pe, 19 + half)
                copied(copy(mix[:, 4 * half:4 * half + 4, :], bank4(2 + half)))
            act.wait_ge(combT_pe, 1)
            for half in range(2):
                last = copy(cT[:, half * S:(half + 1) * S], ps[:, 2 + half, :].bitcast(bf16))
            last.then_inc(combT_done, 1)

            def high(s, cols):
                return copy(roped[:, s // 2, 0, :, cols], turned[:, s % 2, :, :])

            def high_early(s, cols):
                return copy(roped[:, s, 0, :, cols], turned[:, s, :, :])

            with act.Fori(0, PASSES) as w:
                for k in range(PASS_CH):
                    act.wait_ge(up_pe, w * PASS_CH + k + 1)
                    if k >= CH:
                        act.wait_ge(down_pe, w * PASS_CH + k - CH + 1)
                    nc.scalar.activation(hid[:, k % CH, :], ps[:, k % 2, :], ACT.Silu).then_inc(silu_act, 1)
                    for s in range(2):
                        if k == EARLY_ROTARY[2 * s + 1][0] + 3:
                            act.wait_ge(turned_ready, w * 2 + s + 1)
                            high_early(s, bass.ds(w * TB, TB)).then_inc(hi_ready, 1)
                act.wait_ge(down_pe, w * PASS_CH + PASS_CH)

            def softmax_exp(m, count):
                width = (step_of(m)[1] + 1) * P
                act.wait_ge(max_ready, count)
                nc.scalar.activation(probs[:, m % 4, 0:width], sco[m % 2][:, 0:width], ACT.Exp,
                                     bias=negmax[:, m % 4:m % 4 + 1],
                                     accum_out=den[:, m % 4:m % 4 + 1]).then_inc(exp_done, 1)

            def copy_first(m, count):
                width = min(4, step_of(m)[1] + 1) * P
                act.wait_ge(pt_ready, count)
                bank = PT0 + chunks_before(m) % 2
                copy(probsT[:, m % 2, m % 4 // 2, 0:width], ps[:, bank, 0:width]).then_inc(copied_act, 1)

            act.sem_inc(o_free)
            for m in range(S_AHEAD):
                softmax_exp(m, m + 1)
                if m >= S_AHEAD - T_AHEAD:
                    t = m - (S_AHEAD - T_AHEAD)
                    copy_first(t, chunks_before(t) + 1)
            with act.Fori(0, UNITS) as u:
                for j in range(STEPS):
                    if j % 4 >= 2:
                        p, i, _ = step_of(j)
                        act.wait_ge(pv_done, u * 16 + j // 4 * 2 + j % 2 + 1)
                        copy(oT[p][:, i * P:(i + 1) * P], ps[:, OBANK, 0:P]).then_inc(o_free, 1)
                    if j % 2 == 0:
                        softmax_exp(j + S_AHEAD, u * STEPS + j + S_AHEAD + 1)
                    copy_first(j + T_AHEAD, u * CHUNKS + chunks_before(j + T_AHEAD) + 1)
                    if j % 2:
                        softmax_exp(j + S_AHEAD, u * STEPS + j + S_AHEAD + 1)
                    for s in range(4):
                        if HI_AT[s] == j:
                            act.wait_ge(turned_ready, u * 4 + 4 + s + 1)
                            if s == 0:
                                act.wait_ge(in_q[1], u * (16 * Q_STACK_DMAS) + 16 * Q_STACK_DMAS)
                                act.wait_ge(in_k[1], u * (16 * K_STACK_DMAS) + 16 * K_STACK_DMAS)
                            high(s, half_of(s)).then_inc(hi_ready, 1)

        @block.vector
        def _(dve):
            own = [0]

            def then(ins):
                own[0] += 1
                ins.then_inc(dve_own, 1)
                dve.wait_ge(dve_own, own[0])

            for i in range(TILES):
                if i % QB == 0:
                    dve.wait_ge(in_x[i // QB], 16)
                last = nc.vector.bn_stats(stats[:, i, :], acc[:, i, :])
            then(last)
            for i in range(TILES):
                last = nc.vector.bn_aggr(mv[:, i, :], stats[:, i, :])
            then(last)
            nc.vector.tensor_scalar(std[:, 0, :], mv[:, :, 1], EPS, None, ALU.add).then_inc(ln_var, 1)
            dve.wait_ge(ln_std, 1)
            then(nc.vector.reciprocal(std[:, 2, :], std[:, 1, :]))
            then(nc.vector.tensor_tensor(std[:, 3, :], std[:, 0, :], std[:, 2, :], ALU.mult))
            then(nc.vector.tensor_tensor(std[:, 2, :], std[:, 1, :], std[:, 3, :], ALU.add))
            then(nc.vector.tensor_scalar(std[:, 3, :], std[:, 2, :], 0.5, None, ALU.mult))
            then(nc.vector.reciprocal(std[:, 0, :], std[:, 3, :]))
            for i in range(TILES):
                nc.vector.tensor_scalar(xn[:, i, :], acc[:, i, :], mv[:, i, 0:1], std[:, 0, i:i + 1],
                                        ALU.subtract, ALU.mult).then_inc(ln_done, 1)
            for half in range(2):
                dve.wait_ge(first_act, 4 + half)
                for t in range(2):
                    hi = quad_rows(wkT[:, 4 * half:4 * half + 4, 0, :].bitcast(f32), t)
                    last = nc.vector.tensor_tensor(quad_rows(wkT[:, 4 * half:4 * half + 4, 1, :], t),
                                                   halves(3 + half, t), hi, ALU.subtract)
                last.then_inc(first_dve, 1)

            cos, sin = rope[:, 0, :], rope[:, 1, :]

            def turn(slot, t, cols):
                src = ps[:, XBANK, :]
                nc.vector.tensor_tensor(prod[:, slot, 2 * t + 0, :], src, (sin if t else cos)[:, cols], ALU.mult)
                return nc.vector.tensor_tensor(prod[:, slot, 2 * t + 1, :], src, (cos if t else sin)[:, cols],
                                               ALU.mult)

            def low(tensor, slot, cols):
                return nc.vector.tensor_tensor(roped[:, tensor, 1, :, cols], turned[:, slot, :, :],
                                               roped[:, tensor, 0, :, cols].bitcast(f32), ALU.subtract)

            dve.wait_ge(first_act, 12)
            G = TILES * GROUPS
            r_ = [route[:, n, :] for n in range(8)]
            then(nc.vector.tensor_scalar(r_[1], r_[0], 1.0, None, ALU.add))
            then(nc.vector.reciprocal(r_[2], r_[1]))
            four = r_[2].rearrange("p (g a b) -> p g a b", a=2, b=2)
            big, small = r_[3][:, 0:2 * G], r_[3][:, 2 * G:4 * G]
            nc.vector.tensor_tensor(big.rearrange("p (g a) -> p g a", a=2), four[:, :, :, 0], four[:, :, :, 1], ALU.max)
            then(nc.vector.tensor_tensor(small.rearrange("p (g a) -> p g a", a=2), four[:, :, :, 0], four[:, :, :, 1],
                                         ALU.min))
            b2, s2 = big.rearrange("p (g a) -> p g a", a=2), small.rearrange("p (g a) -> p g a", a=2)
            first, a1, a2, second = (r_[4][:, n * G:(n + 1) * G] for n in range(4))
            nc.vector.tensor_tensor(first, b2[:, :, 0], b2[:, :, 1], ALU.max)
            nc.vector.tensor_tensor(a1, b2[:, :, 0], b2[:, :, 1], ALU.min)
            then(nc.vector.tensor_tensor(a2, s2[:, :, 0], s2[:, :, 1], ALU.max))
            then(nc.vector.tensor_tensor(second, a1, a2, ALU.max))
            gsum, grank, gmask = (r_[5][:, n * G:(n + 1) * G] for n in range(3))
            then(nc.vector.tensor_tensor(gsum, first, second, ALU.add))

            def ranks(vals, n, over, ties, low_n, result):
                v = vals.rearrange("p (t e) -> p t e", e=n)
                other = v.unsqueeze(2).broadcast_to([P, TILES, n, n])
                this = v.unsqueeze(3).broadcast_to([P, TILES, n, n])
                nc.vector.tensor_tensor(over, other, this, ALU.is_gt)
                then(nc.vector.tensor_tensor(ties, other, this, ALU.is_equal))
                then(nc.vector.tensor_tensor(ties, ties, low_n.unsqueeze(1).broadcast_to([P, TILES, n, n]), ALU.mult))
                then(nc.vector.tensor_tensor(over, over, ties, ALU.add))
                then(nc.vector.tensor_reduce(result.rearrange("p (t e) -> p t e", e=n), over, AX.X, ALU.add))

            lower4 = lower[:, 0:GROUPS, 0:GROUPS]
            cmp4 = [r_[n].rearrange("p (t a b) -> p t a b", a=GROUPS, b=GROUPS) for n in (6, 7)]
            dve.wait_ge(in_consts, 16 * 3)
            ranks(gsum, GROUPS, cmp4[0], cmp4[1], lower4, grank)
            then(nc.vector.tensor_scalar(gmask, grank, float(TOPG), None, ALU.is_lt))
            masked = r_[1]
            then(nc.vector.tensor_tensor(masked.rearrange("p (g e) -> p g e", e=E // GROUPS),
                                         r_[2].rearrange("p (g e) -> p g e", e=E // GROUPS),
                                         gmask.unsqueeze(2).broadcast_to([P, G, E // GROUPS]), ALU.mult))
            by_tile = [r_[n].rearrange("p (t e) -> p t e", e=E) for n in range(8)]
            for i in range(TILES):
                last = nc.vector.max(top8[:, i, :], by_tile[1][:, i, :])
            then(last)
            fourth = top8[:, :, TOPK - 1:TOPK].broadcast_to([P, TILES, E])
            dve.wait_ge(zeroed, 1)
            nc.vector.tensor_tensor(by_tile[3], by_tile[1], fourth, ALU.is_gt)
            then(nc.vector.tensor_tensor(prefix[:, 0, :, PAD:], by_tile[1], fourth, ALU.is_equal))
            nc.vector.tensor_reduce(r_[7][:, 0:TILES], by_tile[3], AX.X, ALU.add)
            nc.vector.tensor_copy(by_tile[5], prefix[:, 0, :, PAD:])
            shift, at = 1, 0
            while shift < E:
                then(nc.vector.tensor_tensor(prefix[:, 1 - at, :, PAD:], prefix[:, at, :, PAD:],
                                             prefix[:, at, :, PAD - shift:PAD + E - shift], ALU.add))
                shift, at = 2 * shift, 1 - at
            then(nc.vector.tensor_tensor(by_tile[4], prefix[:, at, :, PAD:],
                                         r_[7][:, 0:TILES].unsqueeze(2).broadcast_to([P, TILES, E]), ALU.add))
            then(nc.vector.tensor_scalar(r_[6], r_[4], float(TOPK), None, ALU.is_le))
            then(nc.vector.tensor_tensor(r_[5], r_[5], r_[6], ALU.mult))
            then(nc.vector.tensor_tensor(r_[4], r_[5], r_[3], ALU.add))
            then(nc.vector.tensor_tensor(r_[5], r_[2], r_[4], ALU.mult))
            chosen = r_[5].rearrange("p (t e) -> p t e", e=E)
            then(nc.vector.tensor_reduce(r_[6][:, 0:TILES], chosen, AX.X, ALU.add))
            then(nc.vector.tensor_scalar(r_[6][:, TILES:2 * TILES], r_[6][:, 0:TILES], 1e-20, None, ALU.add))
            then(nc.vector.reciprocal(r_[6][:, 0:TILES], r_[6][:, TILES:2 * TILES]))
            then(nc.vector.tensor_tensor(r_[7].rearrange("p (t e) -> p t e", e=E), chosen,
                                         r_[6][:, 0:TILES].unsqueeze(2).broadcast_to([P, TILES, E]), ALU.mult))
            then(nc.vector.tensor_scalar(r_[0], r_[7], SCALING, None, ALU.mult))
            rest = r_[0]
            for part in range(3):
                to = comb3[:, :, 32 * part:32 * part + E]
                left = rest.rearrange("p (t e) -> p t e", e=E)
                if part == 2:
                    nc.vector.tensor_copy(to, left).then_inc(comb_done, 1)
                else:
                    then(nc.vector.tensor_copy(to, left))
                    nxt = r_[1 + part]
                    then(nc.vector.tensor_tensor(nxt.rearrange("p (t e) -> p t e", e=E), left, to, ALU.subtract))
                    rest = nxt
            def add_down(w, block_):
                dve.wait_ge(down_pe, w * PASS_CH + (block_ + 1) * CH)
                rows = acc[:, bass.ds(w * (2 * TB // P) + block_ * (TB // P), TB // P), :]
                nc.vector.tensor_tensor(rows, rows, ps[:, 4 + block_, :].rearrange("p (c n) -> p c n", c=4),
                                        ALU.add).then_inc(down_added, 1)

            for c in range(4):
                dve.wait_ge(first_act, 13 + c)
                rows, cols = slice(LAT, 2 * LAT), slice(c * TB, (c + 1) * TB)
                nc.vector.tensor_tensor(lT[rows, cols], ps[rows, 4 + c, :], lT[rows, cols].bitcast(f32),
                                        ALU.subtract).then_inc(first_dve, 1)
            dve.wait_ge(in_rope, 16)
            with dve.Fori(0, PASSES) as w:
                half = bass.ds(w * TB, TB)
                for k in range(PASS_CH):
                    if k % CH < ECH:
                        dve.wait_ge(silu_act, w * PASS_CH + k + 1)
                        nc.vector.tensor_tensor(hid[:, k % CH, :], hid[:, k % CH, :], ps[:, 2 + k % 2, :],
                                                ALU.mult).then_inc(gated, 1)
                    for n, (r_at, r) in enumerate(EARLY_ROTARY):
                        if r_at == k:
                            dve.wait_ge(x_ready, w * 4 + n + 1)
                            turn(n // 2, n % 2, half).then_inc(x_free, 1)
                    for s in range(2):
                        if k == EARLY_ROTARY[2 * s + 1][0] + 4:
                            dve.wait_ge(hi_ready, w * 2 + s + 1)
                            low(s, s, half).then_inc(lo_ready, 1)
                    if k == CH + DOWN_LAG:
                        add_down(w, 0)
                add_down(w, 1)
            def row_max(m, count):
                width = (step_of(m)[1] + 1) * P
                dve.wait_ge(s_ready, count)
                nc.vector.tensor_reduce(negmax[:, m % 4:m % 4 + 1], sco[m % 2][:, 0:width], AX.X, ALU.max,
                                        negate=True).then_inc(max_ready, 1)

            def row_rden(m, count):
                dve.wait_ge(exp_done, count)
                nc.vector.reciprocal(rden[:, m % 4:m % 4 + 1], den[:, m % 4:m % 4 + 1]).then_inc(rden_ready, 1)

            def copy_second(m, count):
                width = (step_of(m)[1] + 1 - 4) * P
                bank = PT0 + (chunks_before(m) + 1) % 2
                dve.wait_ge(pt_ready, count)
                nc.vector.tensor_copy(probsT[:, m % 2, m % 4 // 2, TB:TB + width],
                                      ps[:, bank, 0:width]).then_inc(copied_dve, 1)

            def add_projected(use, tile0):
                dve.wait_ge(x_ready, use)
                rows = acc[:, bass.ds(tile0, 4), :]
                nc.vector.tensor_tensor(rows, rows, ps[:, XBANK, :].rearrange("p (c n) -> p c n", c=4),
                                        ALU.add).then_inc(x_free, 1)

            for m in range(S_AHEAD):
                row_max(m, m + 1)
                if m >= 1:
                    row_rden(m - 1, m)
                if m >= S_AHEAD - T_AHEAD:
                    t = m - (S_AHEAD - T_AHEAD)
                    if chunks_of(t) == 2:
                        copy_second(t, chunks_before(t) + 2)
            with dve.Fori(0, UNITS) as u:
                for j in range(STEPS):
                    if j % 2:
                        row_rden(j + S_AHEAD - 1, u * STEPS + j + S_AHEAD)
                    row_max(j + S_AHEAD, u * STEPS + j + S_AHEAD + 1)
                    if j % 2 == 0:
                        row_rden(j + S_AHEAD - 1, u * STEPS + j + S_AHEAD)
                    if chunks_of(j + T_AHEAD) == 2:
                        copy_second(j + T_AHEAD, u * CHUNKS + chunks_before(j + T_AHEAD) + 2)
                    for idx, (at, kind, arg) in enumerate(BANK_USES):
                        if at != j:
                            continue
                        use = u * USES + 8 + idx + 1
                        if kind == "R":
                            dve.wait_ge(x_ready, use)
                            turn(arg // 2 % 2, arg % 2, half_of(arg // 2)).then_inc(x_free, 1)
                        elif arg[0]:
                            add_projected(use, u // (QUADS + 1) * QB + 4 * arg[1])
                        else:
                            add_projected(use, u // QUADS * QB + 4 * arg[1])
                    for s in range(4):
                        if LO_AT[s] == j:
                            dve.wait_ge(hi_ready, u * 4 + 4 + s + 1)
                            low(s // 2, s % 2, half_of(s)).then_inc(lo_ready, 1)
            for half in range(2):
                add_projected(UNITS * USES + 8 + half + 1, (B - 1) * QB + 4 * half)

        @block.gpsimd
        def _(pool):
            nc.gpsimd.memset(comb3[:], 0.0)
            nc.gpsimd.memset(prefix[:, :, :, 0:PAD], 0.0).then_inc(zeroed, 1)
            pool.wait_ge(in_ident, 16)
            nc.gpsimd.tensor_copy(identb[:], ident[:]).then_inc(consts_cast, 1)
            pool.wait_ge(in_consts, 16 * 3)
            nc.gpsimd.tensor_copy(maskb[:], mask_raw[:]).then_inc(consts_cast, 1)
            nc.gpsimd.tensor_copy(sel[:].rearrange("p c n -> p (c n)"), sel_raw[:]).then_inc(consts_cast, 1)

            def rotate_a(s):
                return nc.gpsimd.tensor_tensor(turned[:, s % 2, 0, :], prod[:, s % 2, 0, :], prod[:, s % 2, 2, :],
                                               ALU.subtract)

            def rotate_b(s):
                return nc.gpsimd.tensor_tensor(turned[:, s % 2, 1, :], prod[:, s % 2, 3, :], prod[:, s % 2, 1, :],
                                               ALU.add)

            with pool.Fori(0, PASSES) as w:
                for s in range(2):
                    pool.wait_ge(x_free, w * 4 + 2 * s + 2)
                    rotate_a(s)
                    rotate_b(s).then_inc(turned_ready, 1)
                pool.wait_ge(lo_ready, w * 2 + 2)

            def divide(m, count):
                width = (step_of(m)[1] + 1) * P
                pool.wait_ge(rden_ready, count)
                pool.sem_inc(divide_begun)
                row = probs[:, m % 4, 0:width]
                nc.gpsimd.tensor_scalar(row, row, rden[:, m % 4:m % 4 + 1], 1.0, ALU.mult, ALU.mult)\
                    .then_inc(p_ready, 1)

            pool.wait_ge(combT_pe, 1)
            nc.gpsimd.memset(oT[1][:], 0.0).then_inc(zeroed, 1)
            for m in range(S_AHEAD - 1):
                divide(m, m + 1)
            with pool.Fori(0, UNITS) as u:
                for j in range(STEPS):
                    divide(j + S_AHEAD - 1, u * STEPS + j + S_AHEAD)
                    for s in range(4):
                        if ADD_AT[s][0] == j:
                            upto = [i for i, (_, kind, arg) in enumerate(BANK_USES) if kind == "R" and arg == 2 * s + 1]
                            pool.wait_ge(x_free, u * USES + 8 + upto[0] + 1)
                            rotate_a(s)
                        if ADD_AT[s][1] == j:
                            rotate_b(s).then_inc(turned_ready, 1)


FIRST_JOBS = 20
FIRST_ACT_LAT = 18
FIRST_DVE_WK = 2


def copier_of(k):
    unit, k = k // CHUNKS, k % CHUNKS
    m = n = 0
    while n + chunks_of(m) <= k:
        n += chunks_of(m)
        m += 1
    if k - n:
        return 1, unit * SECONDS + seconds_before(m) + 1, SECONDS
    return 0, unit * STEPS + m + 1, STEPS


def kernel(L0_attn_x, L0_attn_wq, L0_attn_w_kv_down, L0_attn_w_k_up, L0_attn_w_v_up, L0_attn_wo,
           L0_ffn_gate_weight, L0_ffn_expert_up, L0_ffn_expert_down, L0_ffn_shared_up, L0_ffn_shared_down):
    import concourse.bacc as bacc
    from concourse.bass_utils import run_bass_kernel_spmd

    inv_freq = (np.float32(1.0) / np.float32(10000.0) ** (np.arange(0, HD, 2, dtype=np.float32) / np.float32(HD)))
    angle = (np.arange(S, dtype=np.float32)[None, :] * inv_freq[:, None]).astype(np.float32)
    rope = np.stack([np.cos(angle), np.sin(angle)], 1).astype(np.float32)
    rope = np.ascontiguousarray(np.tile(rope, (4, 1, 1)))
    sel = np.zeros((P, ECH, P), np.float32)
    for part in range(3):
        for e in range(E):
            sel[32 * part + e, e // 2, EI * (e % 2):EI * (e % 2) + EI] = 1.0
    lower = np.ascontiguousarray(np.broadcast_to(np.tril(np.ones((E, E), np.float32), -1), (P, E, E)))
    arrays = {
        "x": L0_attn_x, "wq": L0_attn_wq, "w_down": L0_attn_w_kv_down, "w_kup": L0_attn_w_k_up,
        "w_vup": L0_attn_w_v_up, "wo": L0_attn_wo, "gate": L0_ffn_gate_weight, "e_up": L0_ffn_expert_up,
        "e_down": L0_ffn_expert_down, "s_up": L0_ffn_shared_up, "s_down": L0_ffn_shared_down,
        "c_rope": rope, "c_ident": np.eye(P, dtype=np.float32),
        "c_mask": np.triu(np.full((P, P), -1e30, np.float32), 1),
        "c_sel": sel.reshape(P, ECH * P), "c_lower": lower,
    }
    nc = bacc.Bacc("TRN2", target_bir_lowering=False, num_devices=1)
    args = []
    for name in list(arrays):
        a = np.ascontiguousarray(arrays[name])
        arrays[name] = a
        args.append(nc.dram_tensor(name, a.shape, mybir.dt.from_np(a.dtype), kind="ExternalInput").ap())
    args.append(nc.dram_tensor("out", (B, S, D), f32, kind="ExternalOutput").ap())
    block_kernel(nc, *args)
    r = run_bass_kernel_spmd(nc, [arrays], core_ids=[0])
    return r.results[0]["out"]
```

```python
from contextlib import ExitStack

import numpy as np

import concourse.bass as bass
from concourse import mybir

f32 = mybir.dt.float32
f32r = mybir.dt.float32r
bf16 = mybir.dt.bfloat16
ALU = mybir.AluOpType
ACT = mybir.ActivationFunctionType
AX = mybir.AxisListType

P = 128
B, S, D = 2, 1024, 128
HEADS, HD, LAT = 16, 64, 64
TILES = B * S // P
QB = S // P
QUADS = HEADS // 4
UNITS = B * QUADS
HALF = HD // 2
E, EI, SI = 16, 64, 256
CH = (E * EI + SI) // P
ECH = E * EI // P
GROUPS, TOPG, TOPK = 4, 2, 4
SCALING = 2.5
EPS = 1e-5
TB = 512

LONG, SHORT = [7, 6, 5, 4], [0, 1, 2, 3]
STEPS = 4 * QB
S_AHEAD, E_AHEAD, T_AHEAD = 7, 5, 2


def step_of(m):
    m %= STEPS
    return m // (2 * QB), (SHORT if m % 2 else LONG)[m % (2 * QB) // 4], m % 4 // 2


def chunks_of(m):
    return 2 if step_of(m)[1] >= 4 else 1


CHUNKS = sum(chunks_of(m) for m in range(STEPS))
SECONDS = sum(chunks_of(m) - 1 for m in range(STEPS))


def chunks_before(m):
    return m // STEPS * CHUNKS + sum(chunks_of(n) for n in range(m % STEPS))


def seconds_before(m):
    return m // STEPS * SECONDS + sum(chunks_of(n) - 1 for n in range(m % STEPS))


QW = S // 4
PIECES, PROJECTIONS = 8, 8
O_AFTER = 5
R_AT = [0, 0, 2, 2, 3, 4, 6, 7, 8, 10, 11, 12, 14, 15, 16, 18]
ADD_AT, HI_AT, LO_AT = ([R_AT[2 * z + 1] + late for z in range(PIECES)] for late in (0, 2, 2))


def quarter(z):
    return slice(z % 4 * QW, z % 4 * QW + QW)


BANK_USES = sorted([(at, "R", r) for r, at in enumerate(R_AT)] +
                   [((4 * n + O_AFTER) % STEPS, "O", n) for n in range(PROJECTIONS)],
                   key=lambda use: (use[0], use[1] == "R", use[2]))
USES = len(BANK_USES)
LAST_R = max(n for n, use in enumerate(BANK_USES) if use[1] == "R")
FIRST_USES = 2 * PIECES


def uses_at(j, last):
    return [idx for idx, use in enumerate(BANK_USES) if use[0] == j and not (last and use[1] == "R")]


def uses_before(idx, last):
    return sum(not (last and use[1] == "R") for use in BANK_USES[:idx])


ALL_USES = FIRST_USES + (UNITS - 1) * USES + PROJECTIONS + 1
PAD = E // 2
BLOCKS = B * S // TB
PASSES, PASS_CH, DOWN_LAG = B * S // (2 * TB), 2 * ECH, 2
EARLY_PIECES = PIECES // PASSES
Q_STACK_DMAS, K_STACK_DMAS = 16, 4


def block_kernel(nc, x, wq, w_down, w_kup, w_vup, wo, gate, e_up, e_down, s_up, s_down,
                 c_rope, c_ident, c_mask, c_sel, c_lower, out):
    ctx = ExitStack()
    with ctx:
        def sb(name, shape, dt, into=ctx):
            return into.enter_context(nc.sbuf_tensor(name, shape, dt))

        def sem(name):
            return ctx.enter_context(nc.semaphore(name))

        acc = sb("acc", [P, TILES, P], f32)
        rope = sb("rope", [P, 2, S], f32)
        xT = sb("xT", [P, B * S], f32)
        lT = sb("lT", [P, B * S], f32r)
        wqT = sb("wqT", [P, 2 * QUADS, P], f32)
        wkT = sb("wkT", [P, 2 * QUADS, 2, P], f32r)
        wq_now = sb("wq_now", [P, 2, P], f32)
        wk_now = sb("wk_now", [P, 2, 2, P], f32r)
        lat = sb("lat", [P, TILES, LAT], f32)
        lat_now = [sb(f"lat_now{p}", [P, QB, LAT], f32) for p in range(2)]
        mix = sb("mix", [P, HEADS // 2, P], f32)
        ident = sb("ident", [P, P], f32)
        identb = sb("identb", [P, P], bf16)
        mask = sb("mask", [P, S], bf16)
        roped = sb("roped", [P, 2, 2, 2, S], f32r)
        prod = sb("prod", [P, 2, 2, 2, QW], f32)
        turned = sb("turned", [P, 2, 2, QW], f32)
        negmax = sb("negmax", [P, 8], f32)
        den = sb("den", [P, 8], f32)
        rden = sb("rden", [P, 8], f32)

        early = ExitStack()
        with early:
            hid = sb("hid", [P, ECH, TB], f32, early)
            hid_shared = sb("hid_shared", [P, 2, CH - ECH, TB], f32, early)
            shared_out = sb("shared_out", [P, TILES, P], f32, early)
            up = sb("up", [P, CH * P], f32, early)
            down = sb("down", [P, CH, P], f32, early)
            sel = sb("sel", [P, ECH, P], bf16, early)
            cT = sb("cT", [P, B * S], bf16, early)
            xn = sb("xn", [P, TILES, P], f32, early)
            top8 = sb("top8", [P, TILES, 8], f32, early)
            prefix = sb("prefix", [P, 2, TILES, PAD + E], f32, early)
            wq_raw = sb("wq_raw", [P, 2 * QUADS, D], f32, early)
            wk_raw = sb("wk_raw", [P, 2 * QUADS, 2, LAT], f32, early)
            wv_raw = sb("wv_raw", [P, HEADS // 2, LAT], f32, early)
            wo_raw = sb("wo_raw", [P, HEADS // 2, P], f32, early)
            woT = sb("woT", [P, HEADS // 2, P], f32, early)
            comb3 = sb("comb3", [P, TILES, P], bf16, early)
            sel_raw = sb("sel_raw", [P, ECH * P], f32, early)
            lower = sb("lower", [P, E, E], f32, early)
            mask_raw = sb("mask_raw", [P, P], f32, early)
            gate_raw = sb("gate_raw", [E, D], f32, early)
            tokenT = sb("tokenT", [P, LAT + E], f32, early)
            wd_raw = sb("wd_raw", [P, D], f32, early)
            wdT = sb("wdT", [P, P], f32, early)
            stats = sb("stats", [P, TILES, 6], f32, early)
            mv = sb("mv", [P, TILES, 2], f32, early)
            std = sb("std", [P, 4, TILES], f32, early)
            route = sb("route", [P, 8, TILES * E], f32, early)
        probs = [sb("probs_long", [P, 4, S], f32), sb("probs_short", [P, 4, TB], f32)]
        probsT = sb("probsT", [P, 2, 2, S], f32)
        oT = sb("oT", [P, 4, P], f32)
        sb("unused", [P, 6 * 1024 // 4], f32)
        qs = [sb(f"qs{n}", [P, S], f32r) for n in range(4)]
        qx = [sb(f"qx{n}", [P, S], f32r) for n in range(4)]
        ks = [sb(f"ks{n}", [P, S], f32r) for n in range(4)]

        ps = ctx.enter_context(nc.psum_tensor("ps", [P, 8, TB], f32))
        sco = [ps[:, 0:2, :].rearrange("p a n -> p (a n)"), ps[:, 2, :]]
        xbanks = [ps[:, 6, 0:QW], ps[:, 7, 0:QW]]

        def t_bank(m, chunk):
            return 4 if m % 2 or chunk else 3

        def probs_of(m):
            return probs[m % 2][:, m // 2 % 4, :]

        obank = ps[:, 5, 0:P]

        def early_group(n):
            return n // 4 * PIECES + n % 2

        def early_cols(w, piece):
            return bass.ds(w * (2 * QW) + piece % 2 * QW, QW)

        def halves(bank, t):
            return ps[:, bank, :].rearrange("p (g h t j) -> p t g h j", g=2, h=4, t=2)[:, t]

        def quad_rows(weights, t):
            return weights.rearrange("p (g t) (h j) -> p t g h j", t=2, h=4)[:, t]

        in_ident, in_consts, in_small, in_wq, in_wk, in_wv, in_rope, in_exp = map(
            sem, "in_ident in_consts in_small in_wq in_wk in_wv in_rope in_exp".split())
        in_x = [sem("in_x0"), sem("in_x1")]
        zeroed, ln_var, ln_std, ln_done, dve_own = map(sem, "zeroed ln_var ln_std ln_done dve_own".split())
        wk_twice, consts_cast, first_pe, first_act, first_dve = map(
            sem, "wk_twice consts_cast first_pe first_act first_dve".split())
        comb_done, combT_pe, combT_done = map(sem, "comb_done combT_pe combT_done".split())
        up_pe, silu_act, gated, down_pe, added, shared_up, shared_act, shared_down, shared_out_done = map(
            sem, "up_pe silu_act gated down_pe added shared_up shared_act shared_down shared_out_done".split())
        s_ready, max_ready, exp_done, rden_ready, p_ready = map(
            sem, "s_ready max_ready exp_done rden_ready p_ready".split())
        pt_ready, copied_act, copied_dve, pv_done, o_free = map(
            sem, "pt_ready copied_act copied_dve pv_done o_free".split())
        x_ready, x_free, turned_ready, hi_ready, lo_ready = map(
            sem, "x_ready x_free turned_ready hi_ready lo_ready".split())
        in_stage, stored, divide_begun, mask_begun = map(sem, "in_stage stored divide_begun mask_begun".split())
        in_lat = [sem("in_lat0"), sem("in_lat1")]
        in_q = [sem("in_q0"), sem("in_q1")]
        in_k = [sem(f"in_k{n}") for n in range(4)]

        block = ctx.enter_context(nc.Block())

        @block.sync
        def _(sp):
            x_tiles = x.rearrange("b (i p) d -> p (b i) d", p=P)
            for half in range(2):
                tiles = slice(QB * half, QB * half + QB)
                sp.dma_start(acc[:, tiles, :], x_tiles[:, tiles, :]).then_inc(in_x[half], 16)
            sp.dma_start(wk_raw[:, :, 0, :], w_kup.rearrange("(c p) l -> p c l", p=P)).then_inc(in_wk, 16)
            sp.dma_start(lower[:], c_lower).then_inc(in_consts, 16)
            sp.dma_start(mask_raw[:], c_mask).then_inc(in_consts, 16)
            sp.dma_start(sel_raw[:], c_sel).then_inc(in_consts, 16)
            sp.dma_start(down[:, 0:ECH, :], e_down.rearrange("(c f) i h -> (f i) c h", f=2)).then_inc(in_exp, 16)
            sp.dma_start(down[:, ECH:, :], s_down.rearrange("(c p) h -> p c h", p=P)).then_inc(in_exp, 16)
            sp.dma_start(up[:, E * EI:], s_up).then_inc(in_exp, 16)
            sp.dma_start(up[:, 0:E * EI].rearrange("p (e i) -> p e i", i=EI),
                         e_up.rearrange("e h i -> h e i")).then_inc(in_exp, 16)
            sp.dma_start(rope[:], c_rope).then_inc(in_rope, 16)

            def stage_weights(n):
                g = n % QUADS
                sp.dma_start(wq_now[:], wqT[:, bass.ds(2 * g, 2), :]).then_inc(in_stage, 16)
                sp.dma_start(wk_now[:].bitcast(f32), wkT[:, bass.ds(2 * g, 2), :, :].bitcast(f32)).then_inc(in_stage, 16)

            def stage_latent(n, p):
                b = (n // QUADS) % B
                sp.dma_start(lat_now[p][:], lat[:, bass.ds(QB * b, QB), :]).then_inc(in_lat[p], 16)

            def stack(dst, n, tensor, part, place, landed):
                src = roped[HALF * n:HALF * n + HALF, tensor]
                for t in range(2):
                    at = HD * place + HALF * t
                    sp.dma_start(dst[n][at:at + HALF, :].bitcast(f32),
                                 src[:, part, t, :].bitcast(f32)).then_inc(landed, 16)

            def stack_q(p):
                for n in (2 * p, 2 * p + 1):
                    for part in range(2):
                        stack(qs, n, 0, part, part, in_q[p])
                        stack(qx, n, 0, part, 1 - part, in_q[p])

            def stack_k(p, part):
                for n in (2 * p, 2 * p + 1):
                    stack(ks, n, 1, part, part, in_k[n])

            sp.wait_ge(first_act, FIRST_ACT_LAT)
            sp.wait_ge(first_dve, FIRST_DVE_WK)
            stage_weights(0)
            for p in range(2):
                stage_latent(0, p)
            sp.wait_ge(x_ready, FIRST_USES)
            stage_weights(1)
            sp.wait_ge(combT_pe, 1)
            sp.wait_ge(consts_cast, 3)
            sp.wait_ge(first_pe, FIRST_JOBS)
            sp.wait_ge(lo_ready, PIECES)
            for p in range(2):
                stack_q(p)
                for h in range(2):
                    stack_k(p, h)

            def unit_moves(u):
                n = u + 1
                sp.wait_ge(lo_ready, u * PIECES + PIECES + 4)
                sp.wait_ge(s_ready, u * STEPS + 16)
                stack_q(0)
                sp.wait_ge(pv_done, u * 16 + 8)
                stage_latent(n, 0)
                sp.wait_ge(hi_ready, u * PIECES + 2 * PIECES)
                stack_k(0, 0)
                sp.wait_ge(lo_ready, u * PIECES + 2 * PIECES)
                stack_k(0, 1)
                sp.wait_ge(x_ready, u * USES + FIRST_USES + LAST_R + 1)
                stage_weights(n + 1)
                sp.wait_ge(s_ready, u * STEPS + 32)
                stack_q(1)
                stack_k(1, 0)
                stack_k(1, 1)
                sp.wait_ge(pv_done, u * 16 + 16)
                stage_latent(n, 1)

            out_tiles = out.rearrange("b (i p) d -> p (b i) d", p=P)
            with sp.Fori(0, QUADS + 1) as u:
                unit_moves(u)
            sp.wait_ge(x_free, (QUADS + 1) * USES + FIRST_USES)
            sp.dma_start(out_tiles[:, 0:QB, :], acc[:, 0:QB, :]).then_inc(stored, 16)
            with sp.Fori(QUADS + 1, UNITS - 1) as u:
                unit_moves(u)

            sp.wait_ge(x_free, ALL_USES)
            sp.dma_start(out_tiles[:, QB:, :], acc[:, QB:, :]).then_inc(stored, 16)
            sp.wait_ge(stored, 32)

        @block.tensor
        def _(pe):
            def done(ins):
                ins.then_inc(first_pe, 1)

            pe.wait_ge(in_ident, 16)
            pe.wait_ge(in_small, 16 * 3)
            nc.tensor.transpose(ps[:, 0, 0:P], wd_raw[:], ident[:])
            done(nc.tensor.transpose(ps[:, 0, P:P + E], gate_raw[:], ident[0:E, 0:E]))
            pe.wait_ge(in_wq, 16)
            for half in range(2):
                for c in range(4):
                    last = nc.tensor.transpose(ps[:, 1 + half, c * P:(c + 1) * P], wq_raw[:, 4 * half + c, :], ident[:])
                done(last)
            pe.wait_ge(wk_twice, 1)
            for half in range(2):
                for c in range(4):
                    last = nc.tensor.transpose(ps[:, 3 + half, c * P:(c + 1) * P],
                                               wk_raw[:, 4 * half + c, :, :].rearrange("p a l -> p (a l)"), ident[:])
                done(last)
            for b, bank in enumerate((7, 0, 1, 2)):
                pe.wait_ge(ln_done, 4 * (b + 1))
                if b:
                    pe.wait_ge(first_act, b)
                for c in range(4):
                    last = nc.tensor.transpose(ps[:, bank, c * P:(c + 1) * P], xn[:, 4 * b + c, :], ident[:])
                done(last)
            pe.wait_ge(first_act, 9)
            pe.wait_ge(first_dve, 2)
            for i in range(TILES):
                last = nc.tensor.matmul(ps[:, 3 + i // 4, i % 4 * (LAT + E):(i % 4 + 1) * (LAT + E)],
                                        xT[:, i * P:(i + 1) * P], tokenT[:], start=True, stop=True)
            done(last)
            for c, bank in enumerate((7, 0, 1, 2)):
                done(nc.tensor.matmul(ps[:, bank, :], wdT[:], xT[:, c * TB:(c + 1) * TB], start=True, stop=True))
            pe.wait_ge(first_act, 11)
            pe.wait_ge(in_wv, 16 * 2)
            for half in range(2):
                for c in range(4):
                    last = nc.tensor.transpose(ps[:, 5 + half, c * P:(c + 1) * P], wo_raw[:, 4 * half + c, :], ident[:])
                done(last)
            for half in range(2):
                pe.wait_ge(first_act, 16 + half)
                for c in range(4):
                    for a in range(2):
                        rows = slice(HD * a, HD * a + HD)
                        last = nc.tensor.matmul(ps[rows, 3 + half, c * P:(c + 1) * P], wv_raw[rows, 4 * half + c, :],
                                                woT[rows, 4 * half + c, :], start=True, stop=True)
                done(last)

            def rotary_product(r, cols, xbank):
                t = r % 2
                if r < PIECES:
                    last = nc.tensor.matmul(xbank, wq_now[:, t, :], xT[:, cols], start=True, stop=True)
                else:
                    nc.tensor.matmul(xbank, wk_now[:, t, 0, :], lT[:, cols], start=True, stop=False)
                    last = nc.tensor.matmul(xbank, wk_now[:, t, 1, :], lT[:, cols], start=False, stop=True)
                last.then_inc(x_ready, 1)

            pe.wait_ge(in_exp, 64)
            for b in range(BLOCKS + 1):
                for c in range(CH - ECH):
                    if b == BLOCKS:
                        break
                    if b == 0:
                        pe.wait_ge(first_act, 17)
                    else:
                        pe.wait_ge(shared_act, 2 * b + c - 1)
                    nc.tensor.matmul(ps[:, 5 + c, :], up[:, (ECH + c) * P:(ECH + c + 1) * P],
                                     xT[:, b * TB:(b + 1) * TB], start=True, stop=True).then_inc(shared_up, 1)
                if b == 0:
                    continue
                pe.wait_ge(shared_act, 2 * b)
                if b == BLOCKS:
                    pe.wait_ge(consts_cast, 3)
                    pe.wait_ge(comb_done, 1)
                    for i in range(TILES):
                        bank = ps[:, 5 + i // 8, :].bitcast(bf16)
                        last = nc.tensor.transpose(bank[:, i % 8 * P:(i % 8 + 1) * P], comb3[:, i, :], identb[:])
                    last.then_inc(combT_pe, 1)
                if b <= 2:
                    pe.wait_ge(first_act, 17 + b)
                else:
                    pe.wait_ge(shared_out_done, b - 2)
                for i in range(TB // P):
                    for c in range(CH - ECH):
                        last = nc.tensor.matmul(ps[:, 3 + (b - 1) % 2, i * P:(i + 1) * P],
                                                hid_shared[:, (b - 1) % 2, c, i * P:(i + 1) * P],
                                                down[:, ECH + c, :], start=(c == 0), stop=(c == CH - ECH - 1))
                last.then_inc(shared_down, 1)

            pe.wait_ge(first_dve, 6)
            pe.wait_ge(in_stage, 32)
            pe.wait_ge(combT_done, 1)
            pe.wait_ge(shared_out_done, BLOCKS)
            def early_rotary(n, w):
                if n >= 2:
                    pe.wait_ge(x_free, w * (2 * EARLY_PIECES) + n - 1)
                rotary_product(early_group(n), early_cols(w, n // 2), xbanks[n % 2])

            with pe.Fori(0, PASSES) as w:
                for k in range(PASS_CH + DOWN_LAG):
                    if k < PASS_CH:
                        c = k % ECH
                        cols = bass.ds(w * (2 * TB) + k // ECH * TB, TB)
                        if k >= 2:
                            pe.wait_ge(gated, w * PASS_CH + k - 1)
                        nc.tensor.matmul(ps[:, k % 2, :], up[:, c * P:(c + 1) * P], xT[:, cols],
                                         start=True, stop=True)
                        nc.tensor.matmul(ps[:, 2 + k % 2, :], sel[:, c, :], cT[:, cols],
                                         start=True, stop=True).then_inc(up_pe, 1)
                    if k < EARLY_PIECES:
                        early_rotary(2 * k, w)
                    d = k - DOWN_LAG
                    if d >= 0:
                        c = d % ECH
                        pe.wait_ge(gated, w * PASS_CH + d + 1)
                        if d == 0:
                            pe.wait_ge(added, w * 2 + BLOCKS)
                        for i in range(TB // P):
                            last = nc.tensor.matmul(ps[:, 4 + d // ECH, i * P:(i + 1) * P],
                                                    hid[:, c, i * P:(i + 1) * P], down[:, c, :],
                                                    start=(c == 0 and i == 0), stop=(c == ECH - 1 and i == TB // P - 1))
                        last.then_inc(down_pe, 1)
                    if k < EARLY_PIECES:
                        early_rotary(2 * k + 1, w)
                pe.wait_ge(x_free, w * (2 * EARLY_PIECES) + 2 * EARLY_PIECES)

            def scores(m, count):
                p, i, a = step_of(m)
                if count is not None:
                    pe.wait_ge(max_ready, count)
                n, width = 2 * p + a, (i + 1) * P
                rows = slice(i * P, (i + 1) * P)
                out_ps = sco[m % 2]
                for lo in range(0, width, TB):
                    hi = min(lo + TB, max(width, lo + 2 * P))
                    nc.tensor.matmul(out_ps[:, lo:hi], qs[n][:, rows], ks[n][:, lo:hi], start=True, stop=False)
                    last = nc.tensor.matmul(out_ps[:, lo:hi], qx[n][:, rows], ks[n][:, lo:hi], start=False, stop=True)
                last.then_inc(s_ready, 1)

            def transposes(m, u):
                _, i, _ = step_of(m)
                pe.wait_ge(p_ready, u * STEPS + m + 1)
                for x_ in range(chunks_of(m)):
                    if m % 2:
                        pe.wait_ge(copied_dve, u * SECONDS + seconds_before(m))
                    elif x_ == 0:
                        if m >= 2:
                            pe.wait_ge(copied_act, u * STEPS + m - 1)
                    elif m:
                        pe.wait_ge(copied_act, u * STEPS + m)
                    for kb in range(4 * x_, min(4 * x_ + 4, i + 1)):
                        last = nc.tensor.transpose(ps[:, t_bank(m, x_), kb % 4 * P:(kb % 4 + 1) * P],
                                                   probs_of(m)[:, kb * P:(kb + 1) * P], ident[:])
                    last.then_inc(pt_ready, 1)

            def products(m, u):
                p, i, _ = step_of(m)
                k = m // 4 * 2 + m % 2
                if k % 8 == 0:
                    pe.wait_ge(in_lat[p], u * 16 + 16)
                pe.wait_ge(o_free, u * 16 + k + 1)
                pe.wait_ge(copied_act, u * STEPS + m + 1)
                pe.wait_ge(copied_dve, u * SECONDS + seconds_before(m + 1))
                for kb in range(i + 1):
                    for a in range(2):
                        last = nc.tensor.matmul(obank[HD * a:HD * a + HD, :], lat_now[p][:, kb, :],
                                                probsT[:, m % 2, a, kb * P:(kb + 1) * P],
                                                start=(kb == 0), stop=(kb == i))
                last.then_inc(pv_done, 1)

            def project(n, m0, use, outputs, xbank):
                pe.wait_ge(x_free, use - 1)
                pe.wait_ge(o_free, outputs)
                for c in range(2):
                    last = nc.tensor.matmul(xbank[:, c * P:(c + 1) * P], oT[:, (2 * n + 1 - c) % 4, :],
                                            mix[:, m0, :], start=True, stop=True)
                last.then_inc(x_ready, 1)

            def bank_use(idx, u, last):
                _, kind, arg = BANK_USES[idx]
                use = u * USES + FIRST_USES + uses_before(idx, last)
                xbank = xbanks[uses_before(idx, last) % 2]
                if kind == "R":
                    if arg == 0:
                        pe.wait_ge(in_stage, u * 32 + 64)
                    pe.wait_ge(x_free, use - 1)
                    rotary_product(arg, bass.ds((u + 1) // QUADS % B * S + arg // 2 % 4 * QW, QW), xbank)
                elif 4 * arg + O_AFTER < STEPS:
                    project(arg, u % QUADS * 2 + arg // 4, use, u * 16 + 2 * arg + 3, xbank)
                else:
                    project(arg, (u + QUADS - 1) % QUADS * 2 + arg // 4, use, u * 16 + 2 * arg + 3 - 16, xbank)

            pe.wait_ge(in_q[0], 16 * Q_STACK_DMAS)
            for j in range(-S_AHEAD, 0):
                m, t = j + S_AHEAD, j + T_AHEAD
                if m % 2 == 0 and m < 4:
                    pe.wait_ge(in_k[m // 2], 16 * K_STACK_DMAS)
                scores(m, m - 1 if m >= 2 else None)
                if t >= 0:
                    transposes(t, 0)

            def unit(u, last=False):
                for j in range(STEPS):
                    m, t = j + S_AHEAD, j + T_AHEAD
                    if m % 16 in (0, 2) and not (last and m >= STEPS):
                        p, _, a = step_of(m)
                        later = m // STEPS
                        if a == 0:
                            pe.wait_ge(in_q[p], u * (16 * Q_STACK_DMAS) + 16 * Q_STACK_DMAS * (1 + later))
                        pe.wait_ge(in_k[2 * p + a], u * (16 * K_STACK_DMAS) + 16 * K_STACK_DMAS * (1 + later))
                    if not (last and m >= STEPS):
                        scores(m, u * STEPS + m - 1)
                    if j % 4 == 3:
                        products(j, u)
                    if not (last and t >= STEPS):
                        transposes(t, u)
                    if j % 4 == 1:
                        products(j + 1, u)
                    for idx in uses_at(j, last):
                        bank_use(idx, u, last)

            with pe.Fori(0, UNITS - 1) as u:
                unit(u)
            unit(UNITS - 1, last=True)
            project(PROJECTIONS - 1, 2 * QUADS - 1, ALL_USES - 1, 16 * UNITS + 1, xbanks[(ALL_USES - 1) % 2])

        @block.scalar
        def _(act):
            def copy(dst, src, scale=1.0):
                return nc.scalar.activation(dst, src, ACT.Copy, scale=scale)

            def copied(ins):
                ins.then_inc(first_act, 1)

            def bank4(bank):
                return ps[:, bank, :].rearrange("p (c n) -> p c n", c=4)

            act.dma_start(ident[:], c_ident).then_inc(in_ident, 16)
            for half in range(2):
                act.dma_start(wd_raw[LAT * half:LAT * half + LAT, :], w_down).then_inc(in_small, 16)
            act.dma_start(gate_raw[:], gate).then_inc(in_small, 16)
            act.dma_start(wq_raw[:], wq.rearrange("(c p) d -> p c d", p=P)).then_inc(in_wq, 16)
            act.dma_start(wo_raw[:].rearrange("p c r -> p (c r)"), wo).then_inc(in_wv, 16)
            act.dma_start(wv_raw[:], w_vup.rearrange("(c p) l -> p c l", p=P)).then_inc(in_wv, 16)

            act.wait_ge(ln_var, 1)
            nc.scalar.activation(std[:, 1, :], std[:, 0, :], ACT.Sqrt).then_inc(ln_std, 1)
            act.wait_ge(first_pe, 1)
            copy(wdT[:], ps[:, 0, 0:P])
            copy(tokenT[:, 0:LAT], ps[:, 0, 0:LAT])
            copied(copy(tokenT[:, LAT:], ps[:, 0, P:P + E]))
            for half in range(2):
                act.wait_ge(first_pe, 2 + half)
                for t in range(2):
                    last = copy(quad_rows(wqT[:, 4 * half:4 * half + 4, :], t), halves(1 + half, t), HD ** -0.5)
                copied(last)
            for half in range(2):
                act.wait_ge(first_pe, 4 + half)
                for t in range(2):
                    last = copy(quad_rows(wkT[:, 4 * half:4 * half + 4, 0, :], t), halves(3 + half, t))
                copied(last)
            for b, bank in enumerate((7, 0, 1, 2)):
                act.wait_ge(first_pe, 6 + b)
                copied(copy(xT[:, b * TB:(b + 1) * TB], ps[:, bank, :]))
            by_token = ps[:, 3:7, 0:4 * (LAT + E)].rearrange("p b (i n) -> p b i n", i=4)
            act.wait_ge(first_pe, 10)
            copied(nc.scalar.activation(route[:, 0, :].rearrange("p (b i e) -> p b i e", b=4, i=4),
                                        by_token[:, :, :, LAT:], ACT.Exp, scale=-1.0))
            copied(copy(lat[:].rearrange("p (b i) l -> p b i l", i=4), by_token[:, :, :, 0:LAT]))
            for c, bank in enumerate((7, 0, 1, 2)):
                act.wait_ge(first_pe, 11 + c)
                copied(copy(lT[:, c * TB:(c + 1) * TB], ps[:, bank, :]))
            for half in range(2):
                act.wait_ge(first_pe, 15 + half)
                copied(copy(woT[:, 4 * half:4 * half + 4, :], bank4(5 + half)))
            for half in range(2):
                act.wait_ge(first_pe, 17 + half)
                copied(copy(mix[:, 4 * half:4 * half + 4, :], bank4(3 + half)))
            for b in range(BLOCKS + 1):
                for c in range(CH - ECH):
                    if b == BLOCKS:
                        break
                    act.wait_ge(shared_up, 2 * b + c + 1)
                    if b >= 2:
                        act.wait_ge(shared_down, b - 1)
                    nc.scalar.activation(hid_shared[:, b % 2, c, :], ps[:, 5 + c, :], ACT.Silu).then_inc(shared_act, 1)
                if b == BLOCKS:
                    act.wait_ge(combT_pe, 1)
                    for half in range(2):
                        last = copy(cT[:, half * S:(half + 1) * S], ps[:, 5 + half, :].bitcast(bf16))
                    last.then_inc(combT_done, 1)
                if b:
                    act.wait_ge(shared_down, b)
                    copy(shared_out[:, 4 * b - 4:4 * b, :], bank4(3 + (b - 1) % 2)).then_inc(shared_out_done, 1)

            def high(z, cols):
                return copy(roped[:, z // 4, 0, :, cols], turned[:, z % 2, :, :])

            with act.Fori(0, PASSES) as w:
                for k in range(PASS_CH):
                    act.wait_ge(up_pe, w * PASS_CH + k + 1)
                    if k >= ECH:
                        act.wait_ge(down_pe, w * PASS_CH + k - ECH + 1)
                    nc.scalar.activation(hid[:, k % ECH, :], ps[:, k % 2, :], ACT.Silu).then_inc(silu_act, 1)
                    for n in range(EARLY_PIECES):
                        if k == n + 2:
                            act.wait_ge(turned_ready, w * EARLY_PIECES + n + 1)
                            nc.scalar.activation(roped[:, n // 2, 0, :, early_cols(w, n)], turned[:, n % 2, :, :],
                                                 ACT.Copy).then_inc(hi_ready, 1)
                act.wait_ge(down_pe, w * PASS_CH + PASS_CH)

            def softmax_exp(m, count):
                width = (step_of(m)[1] + 1) * P
                act.wait_ge(max_ready, count)
                row = probs_of(m)[:, 0:width]
                nc.scalar.activation(row, row, ACT.Exp, bias=negmax[:, m % 8:m % 8 + 1], scale=-1.0,
                                     accum_out=den[:, m % 8:m % 8 + 1]).then_inc(exp_done, 1)

            def copy_output(k, u):
                act.wait_ge(pv_done, u * 16 + k + 1)
                copy(oT[:, k % 4, :], obank).then_inc(o_free, 1)

            def copy_first(m, count):
                width = min(4, step_of(m)[1] + 1) * P
                act.wait_ge(pt_ready, count)
                copy(probsT[:, m % 2, m % 4 // 2, 0:width], ps[:, t_bank(m, 0), 0:width]).then_inc(copied_act, 1)

            for j in range(-E_AHEAD, 0):
                softmax_exp(j + E_AHEAD, j + E_AHEAD + 1)
                if j + T_AHEAD >= 0:
                    copy_first(j + T_AHEAD, chunks_before(j + T_AHEAD) + 1)

            def unit(u, last=False):
                for j in range(STEPS):
                    if not (last and j + E_AHEAD >= STEPS):
                        softmax_exp(j + E_AHEAD, u * STEPS + j + E_AHEAD + 1)
                    if j % 4 == 3:
                        copy_output(j // 2, u)
                    if not (last and j + T_AHEAD >= STEPS):
                        copy_first(j + T_AHEAD, u * CHUNKS + chunks_before(j + T_AHEAD) + 1)
                    if j % 4 == 1:
                        copy_output(j // 2, u)
                    for z in range(PIECES):
                        if HI_AT[z] == j and not last:
                            act.wait_ge(turned_ready, u * PIECES + PIECES + z + 1)
                            if z == 0:
                                act.wait_ge(in_q[1], u * (16 * Q_STACK_DMAS) + 16 * Q_STACK_DMAS)
                                for head in (2, 3):
                                    act.wait_ge(in_k[head], u * (16 * K_STACK_DMAS) + 16 * K_STACK_DMAS)
                            high(z, quarter(z)).then_inc(hi_ready, 1)

            with act.Fori(0, UNITS - 1) as u:
                unit(u)
            unit(UNITS - 1, last=True)

        @block.vector
        def _(dve):
            own = [0]

            def then(ins):
                own[0] += 1
                ins.then_inc(dve_own, 1)
                dve.wait_ge(dve_own, own[0])

            for i in range(TILES):
                if i % QB == 0:
                    dve.wait_ge(in_x[i // QB], 16)
                last = nc.vector.bn_stats(stats[:, i, :], acc[:, i, :])
            then(last)
            for i in range(TILES):
                last = nc.vector.bn_aggr(mv[:, i, :], stats[:, i, :])
            then(last)
            nc.vector.tensor_scalar(std[:, 0, :], mv[:, :, 1], EPS, None, ALU.add).then_inc(ln_var, 1)
            dve.wait_ge(ln_std, 1)
            then(nc.vector.reciprocal(std[:, 2, :], std[:, 1, :]))
            then(nc.vector.tensor_tensor(std[:, 3, :], std[:, 0, :], std[:, 2, :], ALU.mult))
            then(nc.vector.tensor_tensor(std[:, 2, :], std[:, 1, :], std[:, 3, :], ALU.add))
            then(nc.vector.tensor_scalar(std[:, 3, :], std[:, 2, :], 0.5, None, ALU.mult))
            then(nc.vector.reciprocal(std[:, 0, :], std[:, 3, :]))
            for i in range(TILES):
                nc.vector.tensor_scalar(xn[:, i, :], acc[:, i, :], mv[:, i, 0:1], std[:, 0, i:i + 1],
                                        ALU.subtract, ALU.mult).then_inc(ln_done, 1)
            for half in range(2):
                dve.wait_ge(first_act, 4 + half)
                for t in range(2):
                    hi = quad_rows(wkT[:, 4 * half:4 * half + 4, 0, :].bitcast(f32), t)
                    last = nc.vector.tensor_tensor(quad_rows(wkT[:, 4 * half:4 * half + 4, 1, :], t),
                                                   halves(3 + half, t), hi, ALU.subtract)
                last.then_inc(first_dve, 1)

            def turn(slot, t, cols, xbank):
                return nc.vector.tensor_tensor(prod[:, slot, t, :, :], xbank.unsqueeze(1).broadcast_to([P, 2, QW]),
                                               rope[:, :, cols], ALU.mult)

            def low(tensor, slot, cols):
                return nc.vector.tensor_tensor(roped[:, tensor, 1, :, cols], turned[:, slot, :, :],
                                               roped[:, tensor, 0, :, cols].bitcast(f32), ALU.subtract)

            dve.wait_ge(first_act, 10)
            G = TILES * GROUPS
            r_ = [route[:, n, :] for n in range(8)]
            then(nc.vector.tensor_scalar(r_[1], r_[0], 1.0, None, ALU.add))
            then(nc.vector.reciprocal(r_[2], r_[1]))
            four = r_[2].rearrange("p (g a b) -> p g a b", a=2, b=2)
            big, small = r_[3][:, 0:2 * G], r_[3][:, 2 * G:4 * G]
            nc.vector.tensor_tensor(big.rearrange("p (g a) -> p g a", a=2), four[:, :, :, 0], four[:, :, :, 1], ALU.max)
            then(nc.vector.tensor_tensor(small.rearrange("p (g a) -> p g a", a=2), four[:, :, :, 0], four[:, :, :, 1],
                                         ALU.min))
            b2, s2 = big.rearrange("p (g a) -> p g a", a=2), small.rearrange("p (g a) -> p g a", a=2)
            first, a1, a2, second = (r_[4][:, n * G:(n + 1) * G] for n in range(4))
            nc.vector.tensor_tensor(first, b2[:, :, 0], b2[:, :, 1], ALU.max)
            nc.vector.tensor_tensor(a1, b2[:, :, 0], b2[:, :, 1], ALU.min)
            then(nc.vector.tensor_tensor(a2, s2[:, :, 0], s2[:, :, 1], ALU.max))
            then(nc.vector.tensor_tensor(second, a1, a2, ALU.max))
            gsum, grank, gmask = (r_[5][:, n * G:(n + 1) * G] for n in range(3))
            then(nc.vector.tensor_tensor(gsum, first, second, ALU.add))

            def ranks(vals, n, over, ties, low_n, result):
                v = vals.rearrange("p (t e) -> p t e", e=n)
                other = v.unsqueeze(2).broadcast_to([P, TILES, n, n])
                this = v.unsqueeze(3).broadcast_to([P, TILES, n, n])
                nc.vector.tensor_tensor(over, other, this, ALU.is_gt)
                then(nc.vector.tensor_tensor(ties, other, this, ALU.is_equal))
                then(nc.vector.tensor_tensor(ties, ties, low_n.unsqueeze(1).broadcast_to([P, TILES, n, n]), ALU.mult))
                then(nc.vector.tensor_tensor(over, over, ties, ALU.add))
                then(nc.vector.tensor_reduce(result.rearrange("p (t e) -> p t e", e=n), over, AX.X, ALU.add))

            lower4 = lower[:, 0:GROUPS, 0:GROUPS]
            cmp4 = [r_[n].rearrange("p (t a b) -> p t a b", a=GROUPS, b=GROUPS) for n in (6, 7)]
            dve.wait_ge(in_consts, 16 * 3)
            ranks(gsum, GROUPS, cmp4[0], cmp4[1], lower4, grank)
            then(nc.vector.tensor_scalar(gmask, grank, float(TOPG), None, ALU.is_lt))
            masked = r_[1]
            then(nc.vector.tensor_tensor(masked.rearrange("p (g e) -> p g e", e=E // GROUPS),
                                         r_[2].rearrange("p (g e) -> p g e", e=E // GROUPS),
                                         gmask.unsqueeze(2).broadcast_to([P, G, E // GROUPS]), ALU.mult))
            by_tile = [r_[n].rearrange("p (t e) -> p t e", e=E) for n in range(8)]
            for i in range(TILES):
                last = nc.vector.max(top8[:, i, :], by_tile[1][:, i, :])
            then(last)
            fourth = top8[:, :, TOPK - 1:TOPK].broadcast_to([P, TILES, E])
            dve.wait_ge(zeroed, 1)
            nc.vector.tensor_tensor(by_tile[3], by_tile[1], fourth, ALU.is_gt)
            then(nc.vector.tensor_tensor(prefix[:, 0, :, PAD:], by_tile[1], fourth, ALU.is_equal))
            nc.vector.tensor_reduce(r_[7][:, 0:TILES], by_tile[3], AX.X, ALU.add)
            nc.vector.tensor_copy(by_tile[5], prefix[:, 0, :, PAD:])
            shift, at = 1, 0
            while shift < E:
                then(nc.vector.tensor_tensor(prefix[:, 1 - at, :, PAD:], prefix[:, at, :, PAD:],
                                             prefix[:, at, :, PAD - shift:PAD + E - shift], ALU.add))
                shift, at = 2 * shift, 1 - at
            then(nc.vector.tensor_tensor(by_tile[4], prefix[:, at, :, PAD:],
                                         r_[7][:, 0:TILES].unsqueeze(2).broadcast_to([P, TILES, E]), ALU.add))
            then(nc.vector.tensor_scalar(r_[6], r_[4], float(TOPK), None, ALU.is_le))
            then(nc.vector.tensor_tensor(r_[5], r_[5], r_[6], ALU.mult))
            then(nc.vector.tensor_tensor(r_[4], r_[5], r_[3], ALU.add))
            then(nc.vector.tensor_tensor(r_[5], r_[2], r_[4], ALU.mult))
            chosen = r_[5].rearrange("p (t e) -> p t e", e=E)
            then(nc.vector.tensor_reduce(r_[6][:, 0:TILES], chosen, AX.X, ALU.add))
            then(nc.vector.tensor_scalar(r_[6][:, TILES:2 * TILES], r_[6][:, 0:TILES], 1e-20, None, ALU.add))
            then(nc.vector.reciprocal(r_[6][:, 0:TILES], r_[6][:, TILES:2 * TILES]))
            then(nc.vector.tensor_tensor(r_[7].rearrange("p (t e) -> p t e", e=E), chosen,
                                         r_[6][:, 0:TILES].unsqueeze(2).broadcast_to([P, TILES, E]), ALU.mult))
            then(nc.vector.tensor_scalar(r_[0], r_[7], SCALING, None, ALU.mult))
            rest = r_[0]
            for part in range(3):
                to = comb3[:, :, 32 * part:32 * part + E]
                left = rest.rearrange("p (t e) -> p t e", e=E)
                if part == 2:
                    nc.vector.tensor_copy(to, left).then_inc(comb_done, 1)
                else:
                    then(nc.vector.tensor_copy(to, left))
                    nxt = r_[1 + part]
                    then(nc.vector.tensor_tensor(nxt.rearrange("p (t e) -> p t e", e=E), left, to, ALU.subtract))
                    rest = nxt

            def add_down(w, block_):
                dve.wait_ge(added, BLOCKS)
                dve.wait_ge(down_pe, w * PASS_CH + (block_ + 1) * ECH)
                rows = acc[:, bass.ds(w * (2 * TB // P) + block_ * (TB // P), TB // P), :]
                nc.vector.tensor_tensor(rows, rows, ps[:, 4 + block_, :].rearrange("p (c n) -> p c n", c=4),
                                        ALU.add).then_inc(added, 1)

            def early_turn(n, w):
                dve.wait_ge(x_ready, w * (2 * EARLY_PIECES) + n + 1)
                turn(n // 2 % 2, n % 2, early_cols(w, n // 2), xbanks[n % 2]).then_inc(x_free, 1)

            for c, bank in enumerate((7, 0, 1, 2)):
                dve.wait_ge(first_act, 12 + c)
                rows, cols = slice(LAT, 2 * LAT), slice(c * TB, (c + 1) * TB)
                nc.vector.tensor_tensor(lT[rows, cols], ps[rows, bank, :], lT[rows, cols].bitcast(f32),
                                        ALU.subtract).then_inc(first_dve, 1)
            dve.wait_ge(in_rope, 16)
            with dve.Fori(0, PASSES) as w:
                for k in range(PASS_CH):
                    if k < EARLY_PIECES:
                        if k >= 2:
                            dve.wait_ge(turned_ready, w * EARLY_PIECES + k - 1)
                        early_turn(2 * k, w)
                    dve.wait_ge(silu_act, w * PASS_CH + k + 1)
                    nc.vector.tensor_tensor(hid[:, k % ECH, :], hid[:, k % ECH, :], ps[:, 2 + k % 2, :],
                                            ALU.mult).then_inc(gated, 1)
                    if k < EARLY_PIECES:
                        early_turn(2 * k + 1, w)
                    for n in range(EARLY_PIECES):
                        if k == n + 3:
                            dve.wait_ge(hi_ready, w * EARLY_PIECES + n + 1)
                            low(n // 2, n % 2, early_cols(w, n)).then_inc(lo_ready, 1)
                    if k == ECH + DOWN_LAG:
                        add_down(w, 0)
                add_down(w, 1)
            def row_max(m, count):
                width = (step_of(m)[1] + 1) * P
                dve.wait_ge(s_ready, count)
                dve.sem_inc(mask_begun)
                nc.vector.tensor_tensor_reduce(probs_of(m)[:, 0:width], sco[m % 2][:, 0:width], mask[:, S - width:],
                                               -1.0, 3e38, ALU.add, ALU.min,
                                               accum_out=negmax[:, m % 8:m % 8 + 1]).then_inc(max_ready, 1)

            def row_rden(m, count):
                dve.wait_ge(exp_done, count)
                nc.vector.reciprocal(rden[:, m % 8:m % 8 + 1], den[:, m % 8:m % 8 + 1]).then_inc(rden_ready, 1)

            def copy_second(m, count):
                width = (step_of(m)[1] + 1 - 4) * P
                dve.wait_ge(pt_ready, count)
                nc.vector.tensor_copy(probsT[:, m % 2, m % 4 // 2, TB:TB + width],
                                      ps[:, t_bank(m, 1), 0:width]).then_inc(copied_dve, 1)

            def add_projected(use, n, batch, xbank):
                lower_i, gap = SHORT[n % 4], LONG[n % 4] - SHORT[n % 4]
                dve.wait_ge(x_ready, use)
                rows = acc[:, bass.ds(batch * QB + lower_i, 2, step=gap), :]
                nc.vector.tensor_tensor(rows, rows, xbank.rearrange("p (c n) -> p c n", c=2),
                                        ALU.add).then_inc(x_free, 1)

            def bank_use(idx, u, last):
                _, kind, arg = BANK_USES[idx]
                use = u * USES + FIRST_USES + uses_before(idx, last) + 1
                xbank = xbanks[uses_before(idx, last) % 2]
                if kind == "R":
                    z, t = arg // 2, arg % 2
                    if t == 0:
                        dve.wait_ge(turned_ready, u * PIECES + PIECES + z - 1)
                    dve.wait_ge(x_ready, use)
                    turn(z % 2, t, quarter(z), xbank).then_inc(x_free, 1)
                elif 4 * arg + O_AFTER < STEPS:
                    add_projected(use, arg, u // QUADS, xbank)
                else:
                    add_projected(use, arg, u // (QUADS + 1), xbank)

            for j in range(-S_AHEAD, 0):
                m, e, t = j + S_AHEAD, j + E_AHEAD, j + T_AHEAD
                if t >= 0 and chunks_of(t) == 2:
                    copy_second(t, chunks_before(t) + 2)
                if e >= 0:
                    row_rden(e, e + 1)
                row_max(m, m + 1)

            def unit(u, last=False):
                for j in range(STEPS):
                    m, e, t = j + S_AHEAD, j + E_AHEAD, j + T_AHEAD
                    if not (last and m >= STEPS):
                        row_max(m, u * STEPS + m + 1)
                    if j % 2 and not (last and e >= STEPS):
                        row_rden(e, u * STEPS + e + 1)
                    if j % 2 == 0:
                        if not (last and t >= STEPS):
                            copy_second(t, u * CHUNKS + chunks_before(t) + 2)
                        if not (last and e >= STEPS):
                            row_rden(e, u * STEPS + e + 1)
                    for idx in uses_at(j, last):
                        bank_use(idx, u, last)

            with dve.Fori(0, UNITS - 1) as u:
                unit(u)
            unit(UNITS - 1, last=True)
            add_projected(ALL_USES, PROJECTIONS - 1, B - 1, xbanks[(ALL_USES - 1) % 2])

        @block.gpsimd
        def _(pool):
            pool.wait_ge(in_wk, 16)
            nc.gpsimd.tensor_copy(wk_raw[:, :, 1, :], wk_raw[:, :, 0, :]).then_inc(wk_twice, 1)
            nc.gpsimd.memset(comb3[:], 0.0)
            nc.gpsimd.memset(prefix[:, :, :, 0:PAD], 0.0).then_inc(zeroed, 1)
            pool.wait_ge(in_ident, 16)
            nc.gpsimd.tensor_copy(identb[:], ident[:]).then_inc(consts_cast, 1)
            pool.wait_ge(in_consts, 16 * 3)
            nc.gpsimd.memset(mask[:, 0:S - P], 0.0)
            nc.gpsimd.tensor_copy(mask[:, S - P:], mask_raw[:]).then_inc(consts_cast, 1)
            nc.gpsimd.tensor_copy(sel[:].rearrange("p c n -> p (c n)"), sel_raw[:]).then_inc(consts_cast, 1)

            for b in range(BLOCKS):
                pool.wait_ge(shared_out_done, b + 1)
                rows = acc[:, 4 * b:4 * b + 4, :]
                nc.gpsimd.tensor_tensor(rows, rows, shared_out[:, 4 * b:4 * b + 4, :], ALU.add).then_inc(added, 1)

            def rotate(slot):
                a, b = prod[:, slot, 0], prod[:, slot, 1]
                nc.gpsimd.tensor_tensor(turned[:, slot, 0, :], a[:, 0, :], b[:, 1, :], ALU.subtract)
                nc.gpsimd.tensor_tensor(turned[:, slot, 1, :], b[:, 0, :], a[:, 1, :],
                                        ALU.add).then_inc(turned_ready, 1)

            with pool.Fori(0, PASSES) as w:
                for n in range(EARLY_PIECES):
                    pool.wait_ge(x_free, w * (2 * EARLY_PIECES) + 2 * n + 2)
                    if n >= 2:
                        pool.wait_ge(lo_ready, w * EARLY_PIECES + n - 1)
                    rotate(n % 2)
                pool.wait_ge(lo_ready, w * EARLY_PIECES + EARLY_PIECES)

            def divide(m, count):
                width = (step_of(m)[1] + 1) * P
                pool.wait_ge(rden_ready, count)
                pool.sem_inc(divide_begun)
                row = probs_of(m)[:, 0:width]
                nc.gpsimd.tensor_scalar(row, row, rden[:, m % 8:m % 8 + 1], 1.0, ALU.mult, ALU.mult)\
                    .then_inc(p_ready, 1)

            pool.wait_ge(added, 2 * BLOCKS)
            nc.gpsimd.memset(oT[:], 0.0).then_inc(o_free, 1)
            for m in range(E_AHEAD):
                divide(m, m + 1)

            def unit(u, last=False):
                for j in range(STEPS):
                    if not (last and j + E_AHEAD >= STEPS):
                        divide(j + E_AHEAD, u * STEPS + j + E_AHEAD + 1)
                    for z in range(PIECES):
                        if LO_AT[z] == j and not last:
                            pool.wait_ge(hi_ready, u * PIECES + PIECES + z + 1)
                            nc.gpsimd.tensor_tensor(roped[:, z // 4, 1, :, quarter(z)], turned[:, z % 2, :, :],
                                                    roped[:, z // 4, 0, :, quarter(z)].bitcast(f32),
                                                    ALU.subtract).then_inc(lo_ready, 1)
                    for z in range(PIECES):
                        if ADD_AT[z] == j and not last:
                            upto = BANK_USES.index((R_AT[2 * z + 1], "R", 2 * z + 1))
                            pool.wait_ge(x_free, u * USES + FIRST_USES + upto + 1)
                            pool.wait_ge(lo_ready, u * PIECES + PIECES + z - 1)
                            rotate(z % 2)

            with pool.Fori(0, UNITS - 1) as u:
                unit(u)
            unit(UNITS - 1, last=True)


FIRST_JOBS = 18
FIRST_ACT_LAT = 11
FIRST_DVE_WK = 2


def kernel(L0_attn_x, L0_attn_wq, L0_attn_w_kv_down, L0_attn_w_k_up, L0_attn_w_v_up, L0_attn_wo,
           L0_ffn_gate_weight, L0_ffn_expert_up, L0_ffn_expert_down, L0_ffn_shared_up, L0_ffn_shared_down):
    import concourse.bacc as bacc
    from concourse.bass_utils import run_bass_kernel_spmd

    inv_freq = (np.float32(1.0) / np.float32(10000.0) ** (np.arange(0, HD, 2, dtype=np.float32) / np.float32(HD)))
    angle = (np.arange(S, dtype=np.float32)[None, :] * inv_freq[:, None]).astype(np.float32)
    rope = np.stack([np.cos(angle), np.sin(angle)], 1).astype(np.float32)
    rope = np.ascontiguousarray(np.tile(rope, (4, 1, 1)))
    sel = np.zeros((P, ECH, P), np.float32)
    for part in range(3):
        for e in range(E):
            sel[32 * part + e, e // 2, EI * (e % 2):EI * (e % 2) + EI] = 1.0
    lower = np.ascontiguousarray(np.broadcast_to(np.tril(np.ones((E, E), np.float32), -1), (P, E, E)))
    arrays = {
        "x": L0_attn_x, "wq": L0_attn_wq, "w_down": L0_attn_w_kv_down, "w_kup": L0_attn_w_k_up,
        "w_vup": L0_attn_w_v_up, "wo": L0_attn_wo, "gate": L0_ffn_gate_weight, "e_up": L0_ffn_expert_up,
        "e_down": L0_ffn_expert_down, "s_up": L0_ffn_shared_up, "s_down": L0_ffn_shared_down,
        "c_rope": rope, "c_ident": np.eye(P, dtype=np.float32),
        "c_mask": np.triu(np.full((P, P), -1e30, np.float32), 1),
        "c_sel": sel.reshape(P, ECH * P), "c_lower": lower,
    }
    nc = bacc.Bacc("TRN2", target_bir_lowering=False, num_devices=1)
    args = []
    for name in list(arrays):
        a = np.ascontiguousarray(arrays[name])
        arrays[name] = a
        args.append(nc.dram_tensor(name, a.shape, mybir.dt.from_np(a.dtype), kind="ExternalInput").ap())
    args.append(nc.dram_tensor("out", (B, S, D), f32, kind="ExternalOutput").ap())
    block_kernel(nc, *args)
    r = run_bass_kernel_spmd(nc, [arrays], core_ids=[0])
    return r.results[0]["out"]
```
